# Optimizing a Trainium2 kernel written in Bass

```python
import numpy as np
import jax
import jax.numpy as jnp

def _softmax(x, axis=-1):
    return jax.nn.softmax(x, axis=axis)

def _gelu(x):
    return jax.nn.gelu(x, approximate=True)

def _silu(x):
    return jax.nn.silu(x)

def _sigmoid(x):
    return jax.nn.sigmoid(x)

def _layernorm(x, axis=-1, eps=1e-05):
    m = jnp.mean(x, axis=axis, keepdims=True)
    v = jnp.var(x, axis=axis, keepdims=True)
    return (x - m) / jnp.sqrt(v + eps)

def _scatter_add(tgt, idx, src, axis=0):
    return tgt.at[idx].add(src)

def _segment_sum(src, seg, n):
    return jax.ops.segment_sum(src, seg, n)
kernel_name = 'mk_adj_preln_d1_adj_r2_899471'

def setup_inputs(seed: int=0):
    np.random.seed(seed)
    _w = jnp.asarray

    def _rec_inputs():
        import jax
        import jax.numpy as jnp
        _gk = jax.random.key(seed)
        x = -0.0001071 + 1.001 * jax.random.normal(jax.random.fold_in(_gk, 1), (8, 1500, 64), jnp.float32)
        _a = jax.random.bernoulli(jax.random.fold_in(_gk, 2), 0.00266667, (8, 1500, 1500))
        _a = jnp.logical_or(_a, jnp.swapaxes(_a, -1, -2))
        _a = jnp.logical_or(_a, jnp.eye(1500, dtype=bool))
        _af = _a.astype(jnp.float32)
        adj = _af
        return (x, adj)
    x, adj = _rec_inputs()

    def _L0_gnn_setup():
        import jax, jax.numpy as jnp
        import numpy as np
        B, N, F = (2, 1500, 64)
        H, OUT, ATT = (4, 16, 16)
        DENSITY = 0.01
        key = jax.random.key(seed)
        ks = jax.random.split(key, 6)
        h = jax.random.normal(ks[0], (B, N, F), dtype=jnp.float32)
        a = (jax.random.uniform(ks[1], (B, N, N)) < DENSITY).astype(jnp.float32)
        glorot = lambda k, shape: jax.random.uniform(k, shape, jnp.float32, -1.0, 1.0) * jnp.sqrt(6.0 / (shape[-2] + shape[-1]))
        kernel = glorot(ks[2], (H, F, OUT))
        attention_kernel = glorot(ks[3], (H, F, ATT))
        attention_kernel_2 = glorot(ks[4], (H, F, ATT))
        bias = jax.random.normal(ks[5], (1, 1, H, OUT), dtype=jnp.float32) * 0.01
        return {'h': h, 'a': a, 'kernel': kernel, 'attention_kernel': attention_kernel, 'attention_kernel_2': attention_kernel_2, 'bias': bias}
    _L0_gnn_all = _L0_gnn_setup()
    _L0_gnn_in = {k: v for k, v in _L0_gnn_all.items() if k in ('kernel', 'attention_kernel', 'attention_kernel_2', 'bias')}
    del _L0_gnn_all
    return {'x': x, 'adj': adj, 'L0_gnn_kernel': _L0_gnn_in['kernel'], 'L0_gnn_attention_kernel': _L0_gnn_in['attention_kernel'], 'L0_gnn_attention_kernel_2': _L0_gnn_in['attention_kernel_2'], 'L0_gnn_bias': _L0_gnn_in['bias']}

def reference(x, adj, L0_gnn_kernel, L0_gnn_attention_kernel, L0_gnn_attention_kernel_2, L0_gnn_bias):
    import jax
    import jax.numpy as jnp

    def _L0_gnn_ref(h, a, kernel, attention_kernel, attention_kernel_2, bias):
        import jax, jax.numpy as jnp
        import numpy as np
        B, N, F = (2, 1500, 64)
        H, OUT, ATT = (4, 16, 16)
        DENSITY = 0.01
        feats = jnp.einsum('bnf,hfo->bhno', h, kernel)
        f_self = jnp.einsum('bnf,hfd->hbnd', h, attention_kernel)
        f_other = jnp.einsum('bnf,hfd->hbdn', h, attention_kernel_2)
        a_h = a[None]
        scores = jnp.einsum('hbnd,hbdm->hbnm', f_self, f_other)
        masked = a_h * scores
        masked = jnp.where(masked >= 0, masked, 0.2 * masked)
        masked = masked / jnp.sqrt(jnp.float32(ATT))
        masked = masked + jnp.where(a_h == 0, jnp.float32(-1000000000.0), jnp.float32(0.0))
        attn = jax.nn.softmax(masked, axis=-1)
        attn = attn * jnp.where(a_h == 0, jnp.float32(0.0), jnp.float32(1.0))
        attn = jnp.transpose(attn, (1, 0, 2, 3))
        node_features = jnp.einsum('bhnm,bhmo->bhno', attn, feats)
        node_features = node_features + jnp.transpose(bias, (0, 2, 1, 3))
        node_features = jax.nn.relu(node_features)
        node_features = jnp.transpose(node_features, (0, 2, 1, 3))
        return node_features.reshape(-1, N, H * OUT)
    h = jnp.maximum(_layernorm(x, axis=-1), 0.0)
    x = x + _L0_gnn_ref(h, adj, L0_gnn_kernel, L0_gnn_attention_kernel, L0_gnn_attention_kernel_2, L0_gnn_bias)
    return x

_drawn_inputs = setup_inputs


def setup_inputs(seed=0):
    import zlib

    import numpy as np

    out = dict(_drawn_inputs(seed))
    spreads = {}
    factors = {'L0_gnn_bias': 7.714}
    for name, (base, spread) in spreads.items():
        noise = np.random.default_rng([zlib.crc32(name.encode()), seed]).standard_normal(out[name].shape)
        drawn = base * np.exp(spread * noise) if base else spread * noise
        out[name] = jnp.asarray(drawn.astype(out[name].dtype))
    for name, factor in factors.items():
        out[name] = (out[name] * factor).astype(out[name].dtype)
    return out
```

```python
import numpy as np

B, N, F = 8, 1500, 64
H, D = 4, 16
P = 125
TILES = N // P
CHUNKS = 3
JT = TILES // CHUNKS
CN = JT * P
RING = 3
GROUPS = TILES // RING
UNITS = CHUNKS * TILES
PARTS = 6
KS = PARTS * D
SELF_PART = (0, 0, 0, 1, 1, 2)
OTHER_PART = (0, 1, 2, 0, 1, 0)
OC = D + 1
SLOPE = 0.2
EPS = 1e-5
BIG = float(2 ** 20)
TINY = 1e-30
SAFE = 192.0
BANK = 512
HEAD_STEPS = ("select", "adj_a", "adj_b", "leaky", "mask", "max", "negate", "keep", "recip", "scale")
TILE_STEPS = 1 + H * len(HEAD_STEPS) + 3
MASKED = 1e9
ACT_MASKS = (1, 2)


def gat_program(nc, x, adj, w_feat, w_self, w_other, bias, out):
    import concourse.bass as bass
    from concourse import mybir
    from contextlib import ExitStack

    f32, bf16, i32 = mybir.dt.float32, mybir.dt.bfloat16, mybir.dt.int32
    ALU, ACT, AX = mybir.AluOpType, mybir.ActivationFunctionType, mybir.AxisListType
    ds = bass.ds

    x_v = x.rearrange("b (i p) f -> b p i f", p=P)
    adj_v = adj.rearrange("b (c j p) m -> (b c) p j m", c=CHUNKS, j=JT)
    out_v = out.rearrange("b (c j p) f -> (b c) p j f", c=CHUNKS, j=JT)

    ctx = ExitStack()
    with ctx:
        def sb(name, shape, dt):
            return ctx.enter_context(nc.sbuf_tensor(name, shape, dt))

        def pb(name, shape, dt):
            return ctx.enter_context(nc.psum_tensor(name, shape, dt))

        def sem(name):
            return ctx.enter_context(nc.semaphore(name))

        w_proj = sb("w_proj", [F, 2 * H * D], f32)
        w_f = sb("w_f", [F, H * D], f32)
        bias_bc = sb("bias_bc", [P, H * D], f32)
        ident_f = sb("ident_f", [128, 128], f32)
        ident_b = sb("ident_b", [128, 128], bf16)
        zeros = sb("zeros", [P, BANK], bf16)
        group_of = sb("group_of", [128, 32], bf16)
        half_neg = sb("half_neg", [P, TILES], f32)
        x_sb = sb("x_sb", [P, B, TILES, F], f32)
        sums = sb("sums", [P, TILES], f32)
        mean = sb("mean", [P, TILES], f32)
        var_s = sb("var_s", [P, TILES], f32)
        var_e = sb("var_e", [P, TILES], f32)
        rstd = sb("rstd", [P, TILES], f32)
        centred = sb("centred", [P, TILES, F], f32)
        squared = sb("squared", [P, TILES, F], f32)
        normed = sb("normed", [P, TILES, F], f32)
        hT = sb("hT", [F, N], f32)
        proj = sb("proj", [128, N], f32)
        proj_sq = sb("proj_sq", [128, N], bf16)
        part = sb("part", [128, 3, N], bf16)
        rest = sb("rest", [128, CN], f32)
        self_k = sb("self_k", [KS, 2, H, N], bf16)
        other_k = sb("other_k", [KS, 2, H, N], bf16)
        feats = sb("feats", [P, 2, TILES, H * OC], f32)
        norms = sb("norms", [96, B], f32)
        a_nat = sb("a_nat", [P, 2, JT, N], bf16)
        maskT = sb("maskT", [P, 2, TILES, CN], bf16)
        work = sb("work", [P, RING, H, CN], f32)
        ring_f = sb("ring_f", [P, RING, H, OC], f32)
        acc_sb = sb("acc_sb", [128, CN], f32)
        den = sb("den", [P, JT, H], f32)
        rec = sb("rec", [P, JT, H], f32)
        res = sb("res", [P, JT, H, D], f32)

        pair_a = pb("pair_a", [P, 2, BANK], f32)
        pair_b = pb("pair_b", [P, 2, BANK], f32)
        tr_ps = pb("tr_ps", [P, JT, 256], bf16)
        acc_ps = pb("acc_ps", [128, BANK], f32)
        prep_ps = pb("prep_ps", [128, BANK], f32)
        o_ps = pb("o_ps", [P, JT, 128], f32)

        flag = sb("flag", [1, 1], i32)
        top = sb("top", [96, 1], f32)
        top_all = sb("top_all", [1, 1], f32)
        row_max = sb("row_max", [P, 1], f32)
        neg_max = sb("neg_max", [P, 1], f32)
        row_sum = sb("row_sum", [P, 1], f32)
        row_rec = sb("row_rec", [P, 1], f32)
        work_f = work[:, :, :, :].rearrange("p s h n -> p (s h n)")
        g_prob = work_f[:, 0:N]
        g_adj = work_f[:, N:2 * N]
        g_mask = work_f[:, 2 * N:3 * N]
        g_turned = work_f[:, 3 * N:4 * N]
        g_self = proj[0:F, :]
        g_other = self_k[0:F, :, :, :].rearrange("k s h n -> k (s h n)").bitcast(f32)[:, 0:N]
        g_head = self_k[0:F, :, :, :].rearrange("k s h n -> k (s h n)").bitcast(f32)[:, N:N + P]
        g_feats = feats[:, 0, :, :].rearrange("p m (h o) -> p m h o", h=H)
        g_banks = [pair_a[:, 0, :], pair_a[:, 1, :], pair_b[:, 0, :]]

        self_f = self_k[:, :, :, :].rearrange("k s h n -> k (s h n)")
        other_f = other_k[:, :, :, :].rearrange("k s h n -> k (s h n)")
        a_nat_f = a_nat[:, :, :, :].rearrange("p s j n -> p (s j n)")
        maskT_f = maskT[:, :, :, :].rearrange("p s m n -> p (s m n)")
        feats_f = feats[:, :, :, :].rearrange("p s m c -> p (s m c)")

        const_loaded = sem("const_loaded")
        x_loaded = sem("x_loaded")
        const_made = sem("const_made")
        zero_made = sem("zero_made")
        adj_loaded = sem("adj_loaded")
        ln_v = sem("ln_v")
        ln_g = sem("ln_g")
        prep_made = sem("prep_made")
        prep_read = sem("prep_read")
        split_g = sem("split_g")
        parts_placed = sem("parts_placed")
        a_ready = sem("a_ready")
        b_ready = sem("b_ready")
        a_out = sem("a_out")
        b_out = sem("b_out")
        leaky = sem("leaky")
        probs = sem("probs")
        ring_ready = sem("ring_ready")
        unit_done = sem("unit_done")
        tr_made = sem("tr_made")
        tr_read = sem("tr_read")
        acc_read = sem("acc_read")
        o_made = sem("o_made")
        o_v = sem("o_v")
        o_g = sem("o_g")
        stored = sem("stored")

        top_v = sem("top_v")
        top_turned = sem("top_turned")
        flag_made = sem("flag_made")
        g_ln = sem("g_ln")
        g_rstd = sem("g_rstd")
        g_prep = sem("g_prep")
        g_read = sem("g_read")
        g_loaded = sem("g_loaded")
        g_v = sem("g_v")
        g_scores = sem("g_scores")
        g_exp = sem("g_exp")
        g_turn = sem("g_turn")
        g_copied = sem("g_copied")
        g_out = sem("g_out")
        g_stored = sem("g_stored")
        passed = sem("passed")

        block = ctx.enter_context(nc.Block())

        def U(b, c, m):
            return UNITS * b + TILES * c + m

        def K(b, c):
            return CHUNKS * b + c

        def HT(b, k):
            return 9 * b + k

        def PROJ(b, k):
            return 9 * b + 3 + k

        def FEAT(b, k):
            return 9 * b + 6 + k

        def NORM(b):
            return 9 * b + 8

        def wait(eng, s, value):
            if isinstance(value, int) and value <= 0:
                return
            eng.wait_ge(s, value)
            if not isinstance(value, int) and (eng is nc.gpsimd or eng is nc.sync):
                eng.sem_inc(passed, 1)

        def read_mask(eng, t, k, m):
            to = maskT_f[:, ds((k % 2) * (TILES * CN) + CN * m, CN)].rearrange("p (j n) -> p j n", j=JT)
            wait(eng, tr_made, t + 1)
            if eng is nc.vector:
                ins = nc.vector.tensor_scalar(to, tr_ps[:, :, 0:P], -1.0, BIG, ALU.add, ALU.mult)
            else:
                ins = nc.scalar.activation(to, tr_ps[:, :, 0:P], ACT.Copy, bias=-BIG, scale=BIG)
            ins.then_inc(tr_read, 1)

        def by_flag(eng):
            eng.wait_ge(flag_made, 1)
            return eng.If(eng.value_load(flag[0:1, 0:1], min_val=0, max_val=1) == 1)

        def T(b, i):
            return TILES * b + i

        def VS(t, h, step):
            return TILE_STEPS * t + 1 + len(HEAD_STEPS) * h + HEAD_STEPS.index(step) + 1

        @block.sync
        def _(sp):
            sp.dma_start(x_sb[:, 0, :, :], x_v[0]).then_inc(x_loaded, 16)
            sp.dma_start(w_proj[:, 0:H * D].rearrange("f (h d) -> f h d", h=H),
                         w_self.rearrange("h f d -> f h d")).then_inc(const_loaded, 16)
            sp.dma_start(w_proj[:, H * D:].rearrange("f (h d) -> f h d", h=H),
                         w_other.rearrange("h f d -> f h d")).then_inc(const_loaded, 16)
            sp.dma_start(w_f[:, :].rearrange("f (h d) -> f h d", h=H),
                         w_feat.rearrange("h f d -> f h d")).then_inc(const_loaded, 16)
            sp.dma_start(bias_bc[:, :], bias.rearrange("a b h d -> (a b) (h d)").to_broadcast([P, H * D]))\
              .then_inc(const_loaded, 16)
            sp.wait_ge(x_loaded, 16)
            for b in range(1, B):
                sp.dma_start(x_sb[:, b, :, :], x_v[b]).then_inc(x_loaded, 16)

            def place(b, first=False):
                wait(sp, split_g, 12 * (b + 1))
                if not first:
                    wait(sp, b_ready, U(b - 1, 0, 0) + 1)
                for k in range(PARTS):
                    for side, dst, which in ((0, self_f, SELF_PART), (1, other_f, OTHER_PART)):
                        for h in range(H):
                            sp.dma_start(dst[D * k:D * k + D, ds((b % 2) * (H * N) + h * N, N)],
                                         part[64 * side + D * h:64 * side + D * h + D, which[k], :])\
                              .then_inc(parts_placed, 16)

            def store(b, c):
                wait(sp, o_g, 3 * (K(b, c) + 1))
                k = K(b, c)
                sp.dma_start(out_v[ds(k, 1)].rearrange("o p j f -> (o p) j f"),
                             res[:, :, :, :].rearrange("p j h d -> p j (h d)")).then_inc(stored, 16)

            sp.sem_inc(stored, 16)
            place(0, first=True)
            with sp.Fori(0, B - 1) as b:
                store(b, 0)
                place(b + 1)
                store(b, 1)
                store(b, 2)
            for c in range(CHUNKS):
                store(B - 1, c)
            sp.wait_ge(stored, 16 * (B * CHUNKS + 1))

            with by_flag(sp):
                rows = adj.rearrange("b (i p) m -> (b i) p m", p=P)
                outs = out.rearrange("b (i p) f -> (b i) p f", p=P)

                def load(t):
                    sp.dma_start(g_adj.rearrange("p (o n) -> p o n", o=1), rows[ds(t, 1)].rearrange("o p n -> p o n"))\
                      .then_inc(g_loaded, 16)

                load(0)
                with sp.Fori(0, B * TILES - 1) as t:
                    wait(sp, g_v, TILE_STEPS * (t + 1))
                    sp.dma_start(outs[ds(t, 1)].rearrange("o p f -> (o p) f"),
                                 res[:, 0, :, :].rearrange("p h d -> p (h d)")).then_inc(g_stored, 16)
                    wait(sp, g_stored, 16 * (t + 1))
                    load(t + 1)
                sp.wait_ge(g_v, TILE_STEPS * B * TILES)
                sp.dma_start(outs[B * TILES - 1], res[:, 0, :, :].rearrange("p h d -> p (h d)")).then_inc(g_stored, 16)
                sp.wait_ge(g_stored, 16 * B * TILES)

        @block.gpsimd
        def _(pool):
            def load_adj(k):
                wait(pool, adj_loaded, 32 * k)
                wait(pool, tr_made, TILES * (k - 1))
                for rows in (slice(0, 112), slice(112, P)):
                    pool.dma_start(
                        a_nat_f[rows, ds((k % 2) * (JT * N), JT * N)].rearrange("p (o j n) -> p o j n", o=1, j=JT),
                        adj_v[ds(k, 1)].rearrange("o p j n -> p o j n")[rows]).then_inc(adj_loaded, 16)

            load_adj(0)
            nc.gpsimd.memset(ident_f[:, :], 0.0).then_inc(const_made, 1)
            nc.gpsimd.memset(ident_b[:, :], 0.0).then_inc(const_made, 1)
            nc.gpsimd.memset(group_of[:, 2 * H:], 0.0).then_inc(const_made, 1)
            nc.gpsimd.memset(group_of[:, 0:2 * H], 1.0).then_inc(const_made, 1)
            nc.gpsimd.memset(half_neg[:, :], -0.5).then_inc(const_made, 1)
            pool.wait_ge(const_made, 5)
            nc.gpsimd.affine_select(out=ident_f[:, :], in_=ident_f[:, :], compare_op=ALU.not_equal, fill=1.0,
                                    base=0, pattern=[[-1, 128]], channel_multiplier=1).then_inc(const_made, 1)
            nc.gpsimd.affine_select(out=ident_b[:, :], in_=ident_b[:, :], compare_op=ALU.not_equal, fill=1.0,
                                    base=0, pattern=[[-1, 128]], channel_multiplier=1).then_inc(const_made, 1)
            nc.gpsimd.affine_select(out=group_of[:, 0:2 * H], in_=group_of[:, 0:2 * H], compare_op=ALU.is_ge,
                                    fill=0.0, base=0, pattern=[[-D, 2 * H]], channel_multiplier=1)\
              .then_inc(const_made, 1)
            pool.wait_ge(const_made, 8)
            nc.gpsimd.affine_select(out=group_of[:, 0:2 * H], in_=group_of[:, 0:2 * H], compare_op=ALU.is_ge,
                                    fill=0.0, base=D - 1, pattern=[[D, 2 * H]], channel_multiplier=-1)\
              .then_inc(const_made, 1)

            def norm_centre(b):
                xb = x_sb[:, :, :, :].rearrange("p b i f -> p (b i f)")[:, ds(b * (TILES * F), TILES * F)]\
                    .rearrange("p (i f) -> p i f", i=TILES)
                wait(pool, ln_v, 4 * b + 2)
                wait(pool, prep_made, HT(b - 1, 2) + 1 if isinstance(b, int) is False or b > 0 else 0)
                nc.gpsimd.tensor_tensor(centred[:, :, :], xb, mean[:, :].unsqueeze(2).to_broadcast([P, TILES, F]),
                                        ALU.subtract).then_inc(ln_g, 1)
                wait(pool, ln_g, 4 * b + 1)
                nc.gpsimd.tensor_tensor(squared[:, :, :], centred[:, :, :], centred[:, :, :], ALU.mult)\
                  .then_inc(ln_g, 1)

            def norm_scale(b):
                wait(pool, ln_v, 4 * b + 4)
                nc.gpsimd.tensor_tensor(rstd[:, :], var_e[:, :], half_neg[:, :], ALU.pow).then_inc(ln_g, 1)
                wait(pool, ln_g, 4 * b + 3)
                nc.gpsimd.tensor_tensor(normed[:, :, :], centred[:, :, :],
                                        rstd[:, :].unsqueeze(2).to_broadcast([P, TILES, F]), ALU.mult)\
                  .then_inc(ln_g, 1)

            def split(b, k):
                cols = slice(CN * k, CN * k + CN)
                if k == 0:
                    wait(pool, parts_placed, 16 * 2 * PARTS * H * b)
                wait(pool, prep_read, PROJ(b, k) + 1)
                n = 12 * b + 4 * k
                nc.gpsimd.tensor_copy(part[:, 0, cols], proj[:, cols]).then_inc(split_g, 1)
                wait(pool, split_g, n + 1)
                nc.gpsimd.tensor_tensor(rest[:, :], proj[:, cols], part[:, 0, cols], ALU.subtract).then_inc(split_g, 1)
                wait(pool, split_g, n + 2)
                nc.gpsimd.tensor_copy(part[:, 1, cols], rest[:, :]).then_inc(split_g, 1)
                wait(pool, split_g, n + 3)
                nc.gpsimd.tensor_tensor(part[:, 2, cols], rest[:, :], part[:, 1, cols], ALU.subtract)\
                  .then_inc(split_g, 1)

            def feed(b, c, m, s):
                u = U(b, c, m)
                wait(pool, unit_done, u - RING + 1)
                nc.gpsimd.tensor_copy(ring_f[:, s, :, :].rearrange("p h o -> p (h o)"),
                                      feats_f[:, ds((b % 2) * (TILES * H * OC) + (H * OC) * m, H * OC)])\
                  .then_inc(ring_ready, 1)

            def finish(b, c):
                n = 3 * K(b, c)
                xc = x_sb[:, :, :, :].rearrange("p b i f -> p (b i f)")[:, ds(K(b, c) * (JT * F), JT * F)]
                r = res[:, :, :, :].rearrange("p j h d -> p j (h d)")
                rf = res[:, :, :, :].rearrange("p j h d -> p (j h d)")
                wait(pool, o_v, n + 3)
                nc.gpsimd.tensor_tensor(r, r, bias_bc[:, :].unsqueeze(1).to_broadcast([P, JT, H * D]), ALU.add)\
                  .then_inc(o_g, 1)
                wait(pool, o_g, n + 1)
                nc.gpsimd.tensor_scalar(rf, rf, 0.0, None, ALU.max).then_inc(o_g, 1)
                wait(pool, o_g, n + 2)
                nc.gpsimd.tensor_tensor(rf, rf, xc, ALU.add).then_inc(o_g, 1)

            def head(b, c, first=False, last=False):
                if not (last and c >= 1):
                    load_adj(K(b, c) + 2)
                if c == 0:
                    wait(pool, prep_read, FEAT(b, 1) + 1)
                for s in range(RING):
                    feed(b, c, s, s)
                if not first:
                    finish(*(b, c - 1) if c else (b - 1, CHUNKS - 1))

            def group(b, c, g):
                for s in range(RING):
                    feed(b, c, g * RING + s, s)

            def steady(b, c):
                with pool.Fori(1, GROUPS) as g:
                    group(b, c, g)

            def batch(b, last=False):
                if not last:
                    norm_centre(b + 1)
                with pool.Fori(1, GROUPS - 1) as g:
                    group(b, 0, g)
                if not last:
                    norm_scale(b + 1)
                group(b, 0, GROUPS - 1)
                for c in range(1, CHUNKS):
                    head(b, c, last=last)
                    if c == 1 and not last:
                        for g in range(1, GROUPS):
                            split(b + 1, g - 1)
                            group(b, c, g)
                    else:
                        steady(b, c)

            pool.wait_ge(const_made, 9)
            pool.wait_ge(const_loaded, 64)
            pool.wait_ge(x_loaded, 16)
            norm_centre(0)
            norm_scale(0)
            for k in range(CHUNKS):
                split(0, k)
            load_adj(1)
            head(0, 0, first=True)
            with pool.Fori(0, B - 1) as b:
                batch(b)
                head(b + 1, 0)
            batch(B - 1, last=True)
            finish(B - 1, CHUNKS - 1)

            with by_flag(pool):
                with pool.Fori(0, B) as b:
                    wait(pool, g_ln, 7 * b + 6)
                    nc.gpsimd.tensor_tensor(rstd[:, :], var_e[:, :], half_neg[:, :], ALU.pow).then_inc(g_rstd, 1)

        @block.scalar
        def _(act):
            def read_hT(b, k):
                wait(act, prep_made, HT(b, k) + 1)
                nc.scalar.activation(hT[:, CN * k:CN * k + CN], prep_ps[0:F, 0:CN], ACT.Relu).then_inc(prep_read, 1)

            def read_proj(b, k):
                cols = slice(CN * k, CN * k + CN)
                wait(act, prep_made, PROJ(b, k) + 1)
                wait(act, split_g, 12 * b)
                nc.scalar.activation(proj_sq[:, cols], prep_ps[:, 0:CN], ACT.Square)
                nc.scalar.activation(proj[:, cols], prep_ps[:, 0:CN], ACT.Copy).then_inc(prep_read, 1)

            def read_feats(b, k, first=False):
                half = TILES // 2
                wait(act, prep_made, FEAT(b, k) + 1)
                if not first:
                    wait(act, ring_ready, U(b - 1, 0, 0) + 1)
                if first:
                    act.wait_ge(zero_made, 3)
                dst = feats_f[:, ds((b % 2) * (TILES * H * OC) + k * half * H * OC, half * H * OC)]\
                    .rearrange("p (t o) -> p t o", o=OC)[:, :, 0:D]
                nc.scalar.activation(dst, prep_ps[0:P, 0:half * F].rearrange("p (t o) -> p t o", o=D), ACT.Copy)\
                  .then_inc(prep_read, 1)

            def read_b(b, c, m, s):
                u = U(b, c, m)
                wait(act, b_ready, u + 1)
                wait(act, unit_done, u - RING + 1)
                nc.scalar.activation(work[:, s, 2:4, :], pair_b[:, :, 0:CN], ACT.Copy).then_inc(b_out, 1)

            def exps(u, s):
                wait(act, leaky, u + 1)
                nc.scalar.activation(work[:, s, :, :], work[:, s, :, :], ACT.Exp, scale=0.25).then_inc(probs, 1)

            def read_acc(k):
                wait(act, unit_done, TILES * (k + 1))
                nc.scalar.activation(acc_sb[:, :], acc_ps[:, 0:CN], ACT.Copy).then_inc(acc_read, 1)

            def head(b, c, first=False, last=False):
                for s in range(RING):
                    read_b(b, c, s, s)
                    if s in ACT_MASKS and not (last and c == CHUNKS - 1):
                        read_mask(act, U(b, c, s) + TILES, K(b, c) + 1, s)
                    if c == 1 and not last:
                        for step in (2 * s, 2 * s + 1):
                            if step < 3:
                                read_hT(b + 1, step)
                            else:
                                read_proj(b + 1, step - 3)
                    if c == 2 and not last and s < 2:
                        read_feats(b + 1, s)
                    if not (first and s == 0):
                        exps(U(b, c, s) - 1, (s - 1) % RING)
                    if s == 1 and not first:
                        read_acc(K(b, c) - 1)

            def steady(b, c, last_chunk=False):
                with act.Fori(1, GROUPS) as g:
                    for s in range(RING):
                        m = g * RING + s
                        read_b(b, c, m, s)
                        if s in ACT_MASKS and not last_chunk:
                            read_mask(act, U(b, c, m) + TILES, K(b, c) + 1, m)
                        exps(U(b, c, m) - 1, (s - 1) % RING)

            def batch(b, last=False):
                steady(b, 0)
                for c in range(1, CHUNKS):
                    head(b, c, last=last)
                    steady(b, c, last_chunk=last and c == CHUNKS - 1)

            for k in range(3):
                read_hT(0, k)
            for k in range(3):
                read_proj(0, k)
            for k in range(2):
                read_feats(0, k, first=True)
            head(0, 0, first=True)
            with act.Fori(0, B - 1) as b:
                batch(b)
                head(b + 1, 0)
            batch(B - 1, last=True)
            exps(U(B, 0, 0) - 1, RING - 1)
            read_acc(B * CHUNKS - 1)

            with by_flag(act):
                with act.Fori(0, B) as b:
                    for k in range(3):
                        wait(act, g_prep, 11 * b + k + 1)
                        nc.scalar.activation(hT[:, CN * k:CN * k + CN], prep_ps[0:F, 0:CN], ACT.Relu).then_inc(g_read, 1)
                    for n, to in enumerate((g_self, g_other)):
                        for k in range(3):
                            wait(act, g_prep, 11 * b + 3 * n + k + 4)
                            nc.scalar.activation(to[:, CN * k:CN * k + CN], prep_ps[0:F, 0:CN], ACT.Copy)\
                              .then_inc(g_read, 1)
                    for k in range(2):
                        wait(act, g_prep, 11 * b + k + 10)
                        half = TILES // 2
                        nc.scalar.activation(
                            g_feats[:, half * k:half * k + half, :, 0:D].rearrange("p m h o -> p (m h) o"),
                            prep_ps[0:P, 0:half * F].rearrange("p (t o) -> p t o", o=D), ACT.Copy).then_inc(g_read, 1)
                    with act.Fori(0, TILES) as i:
                        for h in range(H):
                            t = T(b, i)
                            q = H * t + h
                            wait(act, g_v, VS(t, h, "negate"))
                            nc.scalar.activation(g_prob, g_prob, ACT.Exp, bias=neg_max[:, :],
                                                 accum_out=row_sum[:, :]).then_inc(g_exp, 1)
                            wait(act, g_turn, q + 1)
                            for n, bank in enumerate(g_banks):
                                ins = nc.scalar.activation(g_turned[:, CN * n:CN * n + CN], bank[:, 0:CN], ACT.Copy)
                            ins.then_inc(g_copied, 1)

        @block.vector
        def _(dve):
            nc.vector.memset(zeros[:, :], 0.0).then_inc(zero_made, 1)
            nc.vector.memset(feats_f[:, :], 1.0).then_inc(zero_made, 1)
            nc.vector.memset(norms[:, :], 0.0).then_inc(zero_made, 1)

            def norm_sum(b):
                if isinstance(b, int) and b == 0:
                    dve.wait_ge(x_loaded, 16)
                else:
                    dve.wait_ge(x_loaded, 16 * B)
                wait(dve, ln_g, 4 * b)
                xb = x_sb[:, :, :, :].rearrange("p b i f -> p (b i f)")[:, ds(b * (TILES * F), TILES * F)]\
                    .rearrange("p (i f) -> p i f", i=TILES)
                nc.vector.tensor_reduce(sums[:, :], xb, AX.X, ALU.add).then_inc(ln_v, 1)
                wait(dve, ln_v, 4 * b + 1)
                nc.vector.tensor_scalar(mean[:, :], sums[:, :], 1.0 / F, None, ALU.mult).then_inc(ln_v, 1)

            def norm_var(b):
                wait(dve, ln_g, 4 * b + 2)
                nc.vector.tensor_reduce(var_s[:, :], squared[:, :, :], AX.X, ALU.add).then_inc(ln_v, 1)
                wait(dve, ln_v, 4 * b + 3)
                nc.vector.tensor_scalar(var_e[:, :], var_s[:, :], 1.0 / F, EPS, ALU.mult, ALU.add).then_inc(ln_v, 1)

            def unit(b, c, m, s, last_chunk=False):
                u, k = U(b, c, m), K(b, c)
                wait(dve, a_ready, u + 1)
                wait(dve, unit_done, u - RING + 1)
                wait(dve, tr_read, u + 1)
                mask = maskT_f[:, ds((k % 2) * (TILES * CN) + CN * m, CN)]
                nc.vector.tensor_tensor(work[:, s, 0:2, :], pair_a[:, :, 0:CN],
                                        mask.unsqueeze(1).to_broadcast([P, 2, CN]), ALU.add).then_inc(a_out, 1)
                if s not in ACT_MASKS and not last_chunk:
                    read_mask(dve, u + TILES, k + 1, m)
                wait(dve, a_out, u + 1)
                wait(dve, b_out, u + 1)
                w = work[:, s, :, :].rearrange("p h n -> p (h n)")
                nc.vector.scalar_tensor_tensor(w, w, SLOPE, w, ALU.mult, ALU.max).then_inc(leaky, 1)

            def chunk_end(b, c):
                n = 3 * K(b, c)
                o = o_ps[:, :, :].rearrange("p j (h r) -> p j h r", h=H)
                wait(dve, o_made, K(b, c) + 1)
                wait(dve, stored, 16 * (K(b, c) + 1))
                nc.vector.tensor_scalar(den[:, :, :], o[:, :, :, D], TINY, None, ALU.max).then_inc(o_v, 1)
                wait(dve, o_v, n + 1)
                nc.vector.reciprocal(rec[:, :, :], den[:, :, :]).then_inc(o_v, 1)
                wait(dve, o_v, n + 2)
                nc.vector.tensor_tensor(res[:, :, :, :], o[:, :, :, 0:D],
                                        rec[:, :, :].unsqueeze(3).to_broadcast([P, JT, H, D]), ALU.mult)\
                  .then_inc(o_v, 1)

            def read_norm(b):
                wait(dve, prep_made, NORM(b) + 1)
                nc.vector.tensor_reduce(norms[:, ds(b, 1)], prep_ps[0:96, 0:CN], AX.X, ALU.max).then_inc(prep_read, 1)

            def head(b, c, first=False, last=False):
                for s in range(RING):
                    unit(b, c, s, s, last_chunk=last and c == CHUNKS - 1)
                    if c == 0 and s == 0:
                        read_norm(b)
                    if s == 2 and not first:
                        chunk_end(*(b, c - 1) if c else (b - 1, CHUNKS - 1))

            def group(b, c, g, last_chunk=False):
                for s in range(RING):
                    unit(b, c, g * RING + s, s, last_chunk)

            def steady(b, c, last_chunk=False):
                with dve.Fori(1, GROUPS) as g:
                    group(b, c, g, last_chunk)

            def batch(b, last=False):
                if not last:
                    norm_sum(b + 1)
                with dve.Fori(1, GROUPS - 1) as g:
                    group(b, 0, g)
                if not last:
                    norm_var(b + 1)
                group(b, 0, GROUPS - 1)
                for c in range(1, CHUNKS):
                    head(b, c, last=last)
                    steady(b, c, last_chunk=last and c == CHUNKS - 1)

            norm_sum(0)
            norm_var(0)
            dve.wait_ge(zero_made, 3)
            with dve.Fori(0, TILES) as m:
                read_mask(dve, m, 0, m)
            head(0, 0, first=True)
            with dve.Fori(0, B - 1) as b:
                batch(b)
                head(b + 1, 0)
            batch(B - 1, last=True)
            chunk_end(B - 1, CHUNKS - 1)

            nc.vector.tensor_reduce(top[:, :], norms[:, :], AX.X, ALU.max).then_inc(top_v, 1)
            dve.wait_ge(top_turned, 1)
            nc.vector.tensor_reduce(top_all[:, :], prep_ps[0:1, 0:96], AX.X, ALU.max).then_inc(top_v, 1)
            dve.wait_ge(top_v, 2)
            dve.wait_ge(stored, 16 * (B * CHUNKS + 1))
            nc.vector.tensor_scalar(flag[:, :], top_all[:, :], SAFE, None, ALU.is_gt).then_inc(flag_made, 1)

            with by_flag(dve):
                with dve.Fori(0, B) as b:
                    n = 7 * b
                    xb = x_sb[:, :, :, :].rearrange("p b i f -> p (b i f)")[:, ds(b * (TILES * F), TILES * F)]\
                        .rearrange("p (i f) -> p i f", i=TILES)

                    def spread(stat):
                        return stat[:, :].unsqueeze(2).to_broadcast([P, TILES, F])

                    nc.vector.tensor_reduce(sums[:, :], xb, AX.X, ALU.add).then_inc(g_ln, 1)
                    wait(dve, g_ln, n + 1)
                    nc.vector.tensor_scalar(mean[:, :], sums[:, :], 1.0 / F, None, ALU.mult).then_inc(g_ln, 1)
                    wait(dve, g_ln, n + 2)
                    nc.vector.tensor_tensor(centred[:, :, :], xb, spread(mean), ALU.subtract).then_inc(g_ln, 1)
                    wait(dve, g_ln, n + 3)
                    nc.vector.tensor_tensor(squared[:, :, :], centred[:, :, :], centred[:, :, :], ALU.mult)\
                      .then_inc(g_ln, 1)
                    wait(dve, g_ln, n + 4)
                    nc.vector.tensor_reduce(var_s[:, :], squared[:, :, :], AX.X, ALU.add).then_inc(g_ln, 1)
                    wait(dve, g_ln, n + 5)
                    nc.vector.tensor_scalar(var_e[:, :], var_s[:, :], 1.0 / F, EPS, ALU.mult, ALU.add)\
                      .then_inc(g_ln, 1)
                    wait(dve, g_rstd, b + 1)
                    nc.vector.tensor_tensor(normed[:, :, :], centred[:, :, :], spread(rstd), ALU.mult)\
                      .then_inc(g_ln, 1)
                    wait(dve, g_read, 11 * b + 11)
                    dve.sem_inc(passed, 1)
                    with dve.Fori(0, TILES) as i:
                        t = T(b, i)
                        r = res[:, 0, :, :].rearrange("p h d -> p (h d)")
                        x_row = x_sb[:, :, :, :].rearrange("p b i f -> p (b i f)")[:, ds(t * F, F)]
                        wait(dve, g_loaded, 16 * (t + 1))
                        nc.vector.tensor_scalar(g_mask, g_adj, -1.0, MASKED, ALU.add, ALU.mult).then_inc(g_v, 1)
                        for h in range(H):
                            q = H * t + h

                            def done(step):
                                wait(dve, g_v, VS(t, h, step))

                            nc.vector.tensor_scalar(g_head, g_self[:, ds(P * i, P)], group_of[0:F, h:h + 1], None,
                                                    ALU.mult).then_inc(g_v, 1)
                            wait(dve, g_scores, q + 1)
                            nc.vector.tensor_tensor(g_prob[:, 0:2 * CN].rearrange("p (a n) -> p a n", a=2),
                                                    pair_a[:, :, 0:CN],
                                                    g_adj[:, 0:2 * CN].rearrange("p (a n) -> p a n", a=2), ALU.mult)\
                              .then_inc(g_v, 1)
                            nc.vector.tensor_tensor(g_prob[:, 2 * CN:], pair_b[:, 0, 0:CN], g_adj[:, 2 * CN:], ALU.mult)\
                              .then_inc(g_v, 1)
                            done("adj_b")
                            nc.vector.scalar_tensor_tensor(g_prob, g_prob, SLOPE, g_prob, ALU.mult, ALU.max)\
                              .then_inc(g_v, 1)
                            done("leaky")
                            nc.vector.scalar_tensor_tensor(g_prob, g_prob, float(D) ** -0.5, g_mask, ALU.mult, ALU.add)\
                              .then_inc(g_v, 1)
                            done("mask")
                            nc.vector.tensor_reduce(row_max[:, :], g_prob, AX.X, ALU.max).then_inc(g_v, 1)
                            done("max")
                            nc.vector.tensor_scalar(neg_max[:, :], row_max[:, :], -1.0, None, ALU.mult).then_inc(g_v, 1)
                            wait(dve, g_exp, q + 1)
                            nc.vector.tensor_tensor(g_prob, g_prob, g_adj, ALU.mult).then_inc(g_v, 1)
                            nc.vector.reciprocal(row_rec[:, :], row_sum[:, :]).then_inc(g_v, 1)
                            done("recip")
                            wait(dve, g_out, q + 1)
                            nc.vector.tensor_scalar(res[:, 0, h, :], acc_ps[0:P, 0:D], row_rec[:, :], None, ALU.mult)\
                              .then_inc(g_v, 1)
                        end = TILE_STEPS * t + TILE_STEPS - 3
                        wait(dve, g_v, end)
                        nc.vector.tensor_tensor(r, r, bias_bc[:, :], ALU.add).then_inc(g_v, 1)
                        wait(dve, g_v, end + 1)
                        nc.vector.tensor_scalar(r, r, 0.0, None, ALU.max).then_inc(g_v, 1)
                        wait(dve, g_v, end + 2)
                        nc.vector.tensor_tensor(r, r, x_row, ALU.add).then_inc(g_v, 1)

        @block.tensor
        def _(pe):
            mm = nc.tensor.matmul

            def make_hT(b, k):
                wait(pe, prep_read, HT(b, k))
                if not isinstance(b, int):
                    pe.sem_inc(passed, 1)
                for j in range(JT):
                    ins = nc.tensor.transpose(prep_ps[0:F, P * j:P * j + P], normed[:, JT * k + j, :],
                                              ident_f[0:P, 0:P])
                ins.then_inc(prep_made, 1)

            def make_proj(b, k):
                wait(pe, prep_read, PROJ(b, k))
                mm(prep_ps[:, 0:CN], w_proj[:, :], hT[:, CN * k:CN * k + CN], start=True, stop=True)\
                    .then_inc(prep_made, 1)

            def make_feats(b, k):
                wait(pe, prep_read, FEAT(b, k))
                half = TILES // 2
                for t in range(half):
                    i = half * k + t
                    ins = mm(prep_ps[0:P, F * t:F * t + F], hT[:, P * i:P * i + P], w_f[:, :], start=True, stop=True)
                ins.then_inc(prep_made, 1)

            def make_norm(b):
                wait(pe, prep_read, NORM(b))
                for k in range(3):
                    ins = mm(prep_ps[32 * k:32 * k + 32, 0:CN], group_of[:, :], proj_sq[:, CN * k:CN * k + CN],
                             start=True, stop=True)
                ins.then_inc(prep_made, 1)

            def prep(b, step):
                if step < 3:
                    make_hT(b, step)
                else:
                    make_proj(b, step - 3)

            def transpose_mask(t, k, m):
                wait(pe, tr_read, t)
                for j in range(JT):
                    ins = nc.tensor.transpose(tr_ps[:, j, 0:P],
                                              a_nat_f[:, ds((k % 2) * (JT * N) + j * N + P * m, P)],
                                              ident_b[0:P, 0:P])
                ins.then_inc(tr_made, 1)

            def scores(b, c, m):
                u, k = U(b, c, m), K(b, c)
                slot = (b % 2) * (H * N)
                mask = maskT_f[:, ds((k % 2) * (TILES * CN) + CN * m, CN)]

                def head_scores(h, to, stop):
                    return mm(to, other_f[:, ds(slot + h * N + P * m, P)], self_f[:, ds(slot + h * N + CN * c, CN)],
                              start=True, stop=stop)

                wait(pe, a_out, u)
                head_scores(0, pair_a[:, 0, 0:CN], True)
                head_scores(1, pair_a[:, 1, 0:CN], True).then_inc(a_ready, 1)
                wait(pe, b_out, u)
                head_scores(2, pair_b[:, 0, 0:CN], False)
                head_scores(3, pair_b[:, 1, 0:CN], False)
                wait(pe, tr_read, u + 1)
                mm(pair_b[:, 0, 0:CN], ident_b[0:P, 0:P], mask, start=False, stop=True)
                mm(pair_b[:, 1, 0:CN], ident_b[0:P, 0:P], mask, start=False, stop=True).then_inc(b_ready, 1)

            def multiply(u, s, start=False):
                wait(pe, ring_ready, u + 1)
                wait(pe, probs, u + 1)
                if start:
                    mm(acc_ps[:, 0:CN], zeros[:, 0:128], zeros[:, 0:CN], start=True, stop=True)
                for h in range(H):
                    ins = mm(acc_ps[32 * h:32 * h + OC, 0:CN], ring_f[:, s, h, :], work[:, s, h, :],
                             start=False, stop=True, skip_group_check=True)
                ins.then_inc(unit_done, 1)

            def turn_acc(k):
                wait(pe, acc_read, k + 1)
                for j in range(JT):
                    ins = nc.tensor.transpose(o_ps[:, j, :], acc_sb[:, P * j:P * j + P], ident_f[:, :])
                ins.then_inc(o_made, 1)

            def head(b, c, first=False, last=False):
                k = K(b, c)
                if c == 0:
                    wait(pe, parts_placed, 16 * 2 * PARTS * H * (b + 1))
                for s in range(RING):
                    u = U(b, c, s)
                    if c == 1 and not last:
                        if s == 0:
                            wait(pe, ln_g, 4 * (b + 1) + 4)
                        prep(b + 1, 2 * s)
                    scores(b, c, s)
                    if not (last and c == CHUNKS - 1):
                        if s == 0:
                            wait(pe, adj_loaded, 32 * (k + 2))
                        transpose_mask(u + TILES, k + 1, s)
                    if c == 0 and s == 0:
                        make_norm(b)
                    if c == 1 and not last:
                        prep(b + 1, 2 * s + 1)
                    if c == 2 and not last and s < 2:
                        make_feats(b + 1, s)
                    if s < 2:
                        if not first:
                            multiply(u - 2, (s + 1) % RING)
                    else:
                        if not first:
                            turn_acc(k - 1)
                        multiply(u - 2, 0, start=True)

            def steady(b, c, last_chunk=False):
                with pe.Fori(1, GROUPS) as g:
                    for s in range(RING):
                        m = g * RING + s
                        u = U(b, c, m)
                        scores(b, c, m)
                        if not last_chunk:
                            transpose_mask(u + TILES, K(b, c) + 1, m)
                        multiply(u - 2, (s + 1) % RING)

            def batch(b, last=False):
                steady(b, 0)
                for c in range(1, CHUNKS):
                    head(b, c, last=last)
                    steady(b, c, last_chunk=last and c == CHUNKS - 1)

            pe.wait_ge(const_made, 9)
            pe.wait_ge(const_loaded, 64)
            pe.wait_ge(zero_made, 3)
            pe.wait_ge(ln_g, 4)
            for step in range(6):
                prep(0, step)
            for k in range(2):
                make_feats(0, k)
            pe.wait_ge(adj_loaded, 32)
            transpose_mask(0, 0, 0)
            with pe.Fori(1, TILES) as m:
                transpose_mask(m, 0, m)
            head(0, 0, first=True)
            with pe.Fori(0, B - 1) as b:
                batch(b)
                head(b + 1, 0)
            batch(B - 1, last=True)
            multiply(U(B, 0, 0) - 2, 1)
            multiply(U(B, 0, 0) - 1, 2)
            turn_acc(B * CHUNKS - 1)
            pe.wait_ge(top_v, 1)
            mm(prep_ps[0:1, 0:96], top[:, :], ident_f[0:96, 0:96], start=True, stop=True).then_inc(top_turned, 1)

            with by_flag(pe):
                def free(n):
                    wait(pe, g_read, n)
                    pe.sem_inc(passed, 1)

                with pe.Fori(0, B) as b:
                    wait(pe, g_ln, 7 * b + 7)
                    pe.sem_inc(passed, 1)
                    for k in range(3):
                        if k:
                            free(11 * b + k)
                        for j in range(JT):
                            ins = nc.tensor.transpose(prep_ps[0:F, P * j:P * j + P], normed[:, JT * k + j, :],
                                                      ident_f[0:P, 0:P])
                        ins.then_inc(g_prep, 1)
                    for n in range(2):
                        for k in range(3):
                            free(11 * b + 3 * n + k + 3)
                            mm(prep_ps[0:F, 0:CN], w_proj[:, F * n:F * n + F], hT[:, CN * k:CN * k + CN],
                               start=True, stop=True).then_inc(g_prep, 1)
                    for k in range(2):
                        free(11 * b + k + 9)
                        half = TILES // 2
                        for j in range(half):
                            i = half * k + j
                            ins = mm(prep_ps[0:P, F * j:F * j + F], hT[:, P * i:P * i + P], w_f[:, :],
                                     start=True, stop=True)
                        ins.then_inc(g_prep, 1)
                    with pe.Fori(0, TILES) as i:
                        t = T(b, i)
                        for h in range(H):
                            q = H * t + h
                            wait(pe, g_v, VS(t, h, "select"))
                            for n, bank in enumerate(g_banks):
                                ins = mm(bank[:, 0:CN], g_head, g_other[:, CN * n:CN * n + CN], start=True, stop=True)
                            ins.then_inc(g_scores, 1)
                            wait(pe, g_v, VS(t, h, "keep"))
                            for m in range(TILES):
                                ins = nc.tensor.transpose(g_banks[m // JT][:, P * (m % JT):P * (m % JT) + P],
                                                          g_prob[:, P * m:P * m + P], ident_f[0:P, 0:P])
                            ins.then_inc(g_turn, 1)
                            wait(pe, g_copied, q + 1)
                            for m in range(TILES):
                                ins = mm(acc_ps[0:P, 0:D], g_turned[:, P * m:P * m + P], g_feats[:, m, h, 0:D],
                                         start=m == 0, stop=m == TILES - 1)
                            ins.then_inc(g_out, 1)


_INS = ["x", "adj", "L0_gnn_kernel", "L0_gnn_attention_kernel", "L0_gnn_attention_kernel_2", "L0_gnn_bias"]


def kernel(**inputs):
    import concourse.bacc as bacc
    from concourse import mybir
    from concourse.bass_utils import run_bass_kernel_spmd as run

    nc = bacc.Bacc("TRN2", target_bir_lowering=False, num_devices=1)
    arrays, args = {}, []
    for name in _INS:
        a = np.ascontiguousarray(inputs[name])
        arrays[name] = a
        args.append(nc.dram_tensor(name, a.shape, mybir.dt.from_np(a.dtype), kind="ExternalInput").ap())
    args.append(nc.dram_tensor("out", (B, N, H * D), mybir.dt.float32, kind="ExternalOutput").ap())
    gat_program(nc, *args)
    r = run(nc, [arrays], core_ids=[0])
    return r.results[0]["out"]
```

```python
import numpy as np

B, N, F = 8, 1500, 64
H, D = 4, 16
P = 125
TILES = N // P
CHUNKS = 3
JT = TILES // CHUNKS
CN = JT * P
RING = 4
GROUPS = TILES // RING
UNITS = CHUNKS * TILES
PARTS = 6
KS = PARTS * D
SELF_PART = (0, 0, 0, 1, 1, 2)
OTHER_PART = (0, 1, 2, 0, 1, 0)
OC = D + 1
SLOPE = 0.2
EPS = 1e-5
BIG = float(2 ** 20)
TINY = 1e-30
SAFE = 192.0
BANK = 512
HEAD_STEPS = ("select", "adj", "leaky", "mask", "max", "negate", "keep", "recip", "scale")
TILE_STEPS = 1 + H * len(HEAD_STEPS) + 3
EARLY = TILES - 8
PLACED = 16 * 2 * PARTS
MASKED = 1e9
ACT_MASKS = ()


def gat_program(nc, x, adj, w_feat, w_self, w_other, bias, out):
    import concourse.bass as bass
    from concourse import mybir
    from contextlib import ExitStack

    f32, bf16, i32 = mybir.dt.float32, mybir.dt.bfloat16, mybir.dt.int32
    ALU, ACT, AX = mybir.AluOpType, mybir.ActivationFunctionType, mybir.AxisListType
    ds = bass.ds

    part_d = nc.dram_tensor("part_scratch", (2, H, D, 3, N), bf16, kind="Internal").ap()

    x_v = x.rearrange("b (i p) f -> b p i f", p=P)
    adj_v = adj.rearrange("b (c j p) m -> (b c) p j m", c=CHUNKS, j=JT)
    out_v = out.rearrange("b (c j p) f -> (b c) p j f", c=CHUNKS, j=JT)

    ctx = ExitStack()
    with ctx:
        def sb(name, shape, dt):
            return ctx.enter_context(nc.sbuf_tensor(name, shape, dt))

        def pb(name, shape, dt):
            return ctx.enter_context(nc.psum_tensor(name, shape, dt))

        def sem(name):
            return ctx.enter_context(nc.semaphore(name))

        w_proj = sb("w_proj", [F, 2 * H * D], f32)
        w_f = sb("w_f", [F, H * D], f32)
        bias_bc = sb("bias_bc", [P, H * D], f32)
        ident_f = sb("ident_f", [128, 128], f32)
        ident_b = sb("ident_b", [128, 128], bf16)
        zeros = sb("zeros", [P, BANK], bf16)
        group_of = sb("group_of", [128, 32], bf16)
        half_neg = sb("half_neg", [P, TILES], f32)
        x_sb = sb("x_sb", [P, B, TILES, F], f32)
        sums = sb("sums", [P, TILES], f32)
        mean = sb("mean", [P, TILES], f32)
        var_s = sb("var_s", [P, TILES], f32)
        var_e = sb("var_e", [P, TILES], f32)
        rstd = sb("rstd", [P, TILES], f32)
        centred = sb("centred", [P, TILES, F], f32)
        squared = sb("squared", [P, TILES, F], f32)
        normed = sb("normed", [P, TILES, F], f32)
        hT = sb("hT", [F, N], f32)
        proj = sb("proj", [128, N], f32)
        proj_sq = sb("proj_sq", [128, N], bf16)
        part = sb("part", [128, 3, N], bf16)
        rest = sb("rest", [128, CN], f32)
        self_k = sb("self_k", [KS, 2, H, N], bf16)
        other_k = sb("other_k", [KS, 2, H, N], bf16)
        feats = sb("feats", [P, 2, TILES, H * OC], f32)
        norms = sb("norms", [96, B], f32)
        a_nat = sb("a_nat", [P, 2, JT, N], bf16)
        maskT = sb("maskT", [P, 2, TILES, CN], bf16)
        work = sb("work", [P, RING, H, CN], f32)
        ring_f = sb("ring_f", [P, RING, H, OC], f32)
        acc_sb = sb("acc_sb", [128, CN], f32)
        den = sb("den", [P, JT, H], f32)
        rec = sb("rec", [P, JT, H], f32)
        res = sb("res", [P, JT, H, D], f32)

        bank_a = pb("bank_a", [P, BANK], f32)
        banks_b = pb("banks_b", [P, H - 1, BANK], f32)
        tr_ps = pb("tr_ps", [P, JT, 256], bf16)
        acc_ps = pb("acc_ps", [128, BANK], f32)
        prep_ps = pb("prep_ps", [128, BANK], f32)
        o_ps = pb("o_ps", [P, JT, 128], f32)

        flag = sb("flag", [1, 1], i32)
        top = sb("top", [96, 1], f32)
        top_all = sb("top_all", [1, 1], f32)
        row_max = sb("row_max", [P, 1], f32)
        neg_max = sb("neg_max", [P, 1], f32)
        row_sum = sb("row_sum", [P, 1], f32)
        row_rec = sb("row_rec", [P, 1], f32)
        work_f = work[:, :, :, :].rearrange("p s h n -> p (s h n)")
        g_prob = work_f[:, 0:N]
        g_adj = work_f[:, N:2 * N]
        g_mask = work_f[:, 2 * N:3 * N]
        g_turned = work_f[:, 3 * N:4 * N]
        g_self = proj[0:F, :]
        g_other = self_k[0:F, :, :, :].rearrange("k s h n -> k (s h n)").bitcast(f32)[:, 0:N]
        g_head = self_k[0:F, :, :, :].rearrange("k s h n -> k (s h n)").bitcast(f32)[:, N:N + P]
        g_feats = feats[:, 0, :, :].rearrange("p m (h o) -> p m h o", h=H)
        g_banks = banks_b[:, :, 0:CN]

        self_f = self_k[:, :, :, :].rearrange("k s h n -> k (s h n)")
        other_f = other_k[:, :, :, :].rearrange("k s h n -> k (s h n)")
        a_nat_f = a_nat[:, :, :, :].rearrange("p s j n -> p (s j n)")
        maskT_f = maskT[:, :, :, :].rearrange("p s m n -> p (s m n)")
        feats_f = feats[:, :, :, :].rearrange("p s m c -> p (s m c)")

        const_loaded = sem("const_loaded")
        x_loaded = sem("x_loaded")
        const_made = sem("const_made")
        zero_made = sem("zero_made")
        adj_loaded = sem("adj_loaded")
        ln_v = sem("ln_v")
        ln_g = sem("ln_g")
        prep_made = sem("prep_made")
        prep_read = sem("prep_read")
        split_g = sem("split_g")
        parts_out = sem("parts_out")
        parts_placed = sem("parts_placed")
        a_ready = sem("a_ready")
        b_ready = sem("b_ready")
        a_out = sem("a_out")
        b_out = sem("b_out")
        leaky = sem("leaky")
        probs = sem("probs")
        ring_ready = sem("ring_ready")
        unit_done = sem("unit_done")
        tr_made = sem("tr_made")
        tr_read = sem("tr_read")
        acc_read = sem("acc_read")
        o_made = sem("o_made")
        o_v = sem("o_v")
        o_g = sem("o_g")
        stored = sem("stored")

        top_v = sem("top_v")
        top_turned = sem("top_turned")
        flag_made = sem("flag_made")
        g_ln = sem("g_ln")
        g_rstd = sem("g_rstd")
        g_prep = sem("g_prep")
        g_read = sem("g_read")
        g_loaded = sem("g_loaded")
        g_v = sem("g_v")
        g_scores = sem("g_scores")
        g_exp = sem("g_exp")
        g_turn = sem("g_turn")
        g_copied = sem("g_copied")
        g_out = sem("g_out")
        g_stored = sem("g_stored")
        passed = sem("passed")

        block = ctx.enter_context(nc.Block())

        def U(b, c, m):
            return UNITS * b + TILES * c + m

        def K(b, c):
            return CHUNKS * b + c

        def HT(b, k):
            return 9 * b + 2 * k

        def PROJ(b, k):
            return 9 * b + 2 * k + 1

        def FEAT(b, k):
            return 9 * b + 6 + k

        def NORM(b):
            return 9 * b + 8

        def wait(eng, s, value):
            if isinstance(value, int) and value <= 0:
                return
            eng.wait_ge(s, value)
            if not isinstance(value, int) and (eng is nc.gpsimd or eng is nc.sync):
                eng.sem_inc(passed, 1)

        def read_mask(eng, t, k, m):
            to = maskT_f[:, ds((k % 2) * (TILES * CN) + CN * m, CN)].rearrange("p (j n) -> p j n", j=JT)
            wait(eng, tr_made, t + 1)
            if eng is nc.vector:
                ins = nc.vector.tensor_scalar(to, tr_ps[:, :, 0:P], -1.0, BIG, ALU.add, ALU.mult)
            else:
                ins = nc.scalar.activation(to, tr_ps[:, :, 0:P], ACT.Copy, bias=-BIG, scale=BIG)
            ins.then_inc(tr_read, 1)

        def by_flag(eng):
            eng.wait_ge(flag_made, 1)
            return eng.If(eng.value_load(flag[0:1, 0:1], min_val=0, max_val=1) == 1)

        def all_stored(eng):
            eng.wait_ge(stored, 16 * (B * CHUNKS + 1))

        def T(b, i):
            return TILES * b + i

        def VS(t, h, step):
            return TILE_STEPS * t + 1 + len(HEAD_STEPS) * h + HEAD_STEPS.index(step) + 1

        def norm_centre(eng, b):
            xb = x_sb[:, :, :, :].rearrange("p b i f -> p (b i f)")[:, ds(b * (TILES * F), TILES * F)]\
                .rearrange("p (i f) -> p i f", i=TILES)
            wait(eng, ln_v, 4 * b + 2)
            wait(eng, prep_made, HT(b - 1, 2) + 1)
            eng.tensor_tensor(centred[:, :, :], xb, mean[:, :].unsqueeze(2).to_broadcast([P, TILES, F]),
                              ALU.subtract).then_inc(ln_g, 1)
            wait(eng, ln_g, 4 * b + 1)
            eng.tensor_tensor(squared[:, :, :], centred[:, :, :], centred[:, :, :], ALU.mult).then_inc(ln_g, 1)

        def norm_rstd(b):
            wait(nc.gpsimd, ln_v, 4 * b + 4)
            nc.gpsimd.tensor_tensor(rstd[:, :], var_e[:, :], half_neg[:, :], ALU.pow).then_inc(ln_g, 1)

        def norm_scale(eng, b):
            wait(eng, ln_g, 4 * b + 3)
            eng.tensor_tensor(normed[:, :, :], centred[:, :, :],
                              rstd[:, :].unsqueeze(2).to_broadcast([P, TILES, F]), ALU.mult).then_inc(ln_g, 1)

        def split(eng, b, k):
            cols = slice(CN * k, CN * k + CN)
            if k == 0 and not isinstance(b, int):
                wait(eng, parts_out, 16 * (b - 1 + CHUNKS))
            wait(eng, prep_read, PROJ(b, k) + 1)
            n = 12 * b + 4 * k
            eng.tensor_copy(part[:, 0, cols], proj[:, cols]).then_inc(split_g, 1)
            wait(eng, split_g, n + 1)
            eng.tensor_tensor(rest[:, :], proj[:, cols], part[:, 0, cols], ALU.subtract).then_inc(split_g, 1)
            wait(eng, split_g, n + 2)
            eng.tensor_copy(part[:, 1, cols], rest[:, :]).then_inc(split_g, 1)
            wait(eng, split_g, n + 3)
            eng.tensor_tensor(part[:, 2, cols], rest[:, :], part[:, 1, cols], ALU.subtract).then_inc(split_g, 1)

        def finish(eng, b, c):
            n = 3 * K(b, c)
            xc = x_sb[:, :, :, :].rearrange("p b i f -> p (b i f)")[:, ds(K(b, c) * (JT * F), JT * F)]
            r = res[:, :, :, :].rearrange("p j h d -> p j (h d)")
            rf = res[:, :, :, :].rearrange("p j h d -> p (j h d)")
            wait(eng, o_v, n + 3)
            eng.tensor_tensor(r, r, bias_bc[:, :].unsqueeze(1).to_broadcast([P, JT, H * D]), ALU.add)\
              .then_inc(o_g, 1)
            wait(eng, o_g, n + 1)
            eng.tensor_scalar(rf, rf, 0.0, None, ALU.max).then_inc(o_g, 1)
            wait(eng, o_g, n + 2)
            eng.tensor_tensor(rf, rf, xc, ALU.add).then_inc(o_g, 1)

        @block.sync
        def _(sp):
            sp.dma_start(x_sb[:, 0, :, :], x_v[0]).then_inc(x_loaded, 16)
            sp.dma_start(w_proj[:, 0:H * D].rearrange("f (h d) -> f h d", h=H),
                         w_self.rearrange("h f d -> f h d")).then_inc(const_loaded, 16)
            sp.dma_start(w_proj[:, H * D:].rearrange("f (h d) -> f h d", h=H),
                         w_other.rearrange("h f d -> f h d")).then_inc(const_loaded, 16)
            sp.dma_start(w_f[:, :].rearrange("f (h d) -> f h d", h=H),
                         w_feat.rearrange("h f d -> f h d")).then_inc(const_loaded, 16)
            sp.dma_start(bias_bc[:, :], bias.rearrange("a b h d -> (a b) (h d)").to_broadcast([P, H * D]))\
              .then_inc(const_loaded, 16)
            sp.wait_ge(x_loaded, 16)
            for b in range(1, B):
                sp.dma_start(x_sb[:, b, :, :], x_v[b]).then_inc(x_loaded, 16)

            def place(b, k=None):
                cols = slice(0, N) if k is None else slice(CN * k, CN * k + CN)
                wait(sp, split_g, 12 * (b + 1) if k is None else 4 * (k + 1))
                if k is None:
                    wait(sp, b_ready, U(b - 1, 0, 0) + 1)
                sp.dma_start(part_d.rearrange("s h d w n -> (s h d) w n")[:, :, cols], part[:, :, cols])\
                  .then_inc(parts_out, 16)
                wait(sp, parts_out, 16 * (b + CHUNKS if k is None else k + 1))
                for n in range(PARTS):
                    for side, dst, which in ((0, self_f, SELF_PART), (1, other_f, OTHER_PART)):
                        sp.dma_start(
                            dst[D * n:D * n + D, ds((b % 2) * (H * N), H * N)]
                            .rearrange("d (h n) -> d h n", h=H)[:, :, cols],
                            part_d[side, :, :, which[n], cols].rearrange("h d n -> d h n")).then_inc(parts_placed, 16)

            def store(b, c):
                wait(sp, o_g, 3 * (K(b, c) + 1))
                k = K(b, c)
                sp.dma_start(out_v[ds(k, 1)].rearrange("o p j f -> (o p) j f"),
                             res[:, :, :, :].rearrange("p j h d -> p j (h d)")).then_inc(stored, 16)

            sp.sem_inc(stored, 16)
            for k in range(CHUNKS):
                place(0, k)
            with sp.Fori(0, B - 1) as b:
                store(b, 0)
                place(b + 1)
                store(b, 1)
                store(b, 2)
            for c in range(CHUNKS):
                store(B - 1, c)
            sp.wait_ge(stored, 16 * (B * CHUNKS + 1))

            with by_flag(sp):
                rows = adj.rearrange("b (i p) m -> (b i) p m", p=P)
                outs = out.rearrange("b (i p) f -> (b i) p f", p=P)

                def load(t):
                    sp.dma_start(g_adj.rearrange("p (o n) -> p o n", o=1), rows[ds(t, 1)].rearrange("o p n -> p o n"))\
                      .then_inc(g_loaded, 16)

                load(0)
                with sp.Fori(0, B * TILES - 1) as t:
                    wait(sp, g_v, TILE_STEPS * (t + 1))
                    sp.dma_start(outs[ds(t, 1)].rearrange("o p f -> (o p) f"),
                                 res[:, 0, :, :].rearrange("p h d -> p (h d)")).then_inc(g_stored, 16)
                    wait(sp, g_stored, 16 * (t + 1))
                    load(t + 1)
                sp.wait_ge(g_v, TILE_STEPS * B * TILES)
                sp.dma_start(outs[B * TILES - 1], res[:, 0, :, :].rearrange("p h d -> p (h d)")).then_inc(g_stored, 16)
                sp.wait_ge(g_stored, 16 * B * TILES)

        @block.gpsimd
        def _(pool):
            def load_adj(k):
                wait(pool, adj_loaded, 32 * k)
                wait(pool, tr_made, TILES * (k - 1))
                for rows in (slice(0, 112), slice(112, P)):
                    pool.dma_start(
                        a_nat_f[rows, ds((k % 2) * (JT * N), JT * N)].rearrange("p (o j n) -> p o j n", o=1, j=JT),
                        adj_v[ds(k, 1)].rearrange("o p j n -> p o j n")[rows]).then_inc(adj_loaded, 16)

            load_adj(0)
            nc.gpsimd.memset(ident_f[:, :], 0.0).then_inc(const_made, 1)
            nc.gpsimd.memset(ident_b[:, :], 0.0).then_inc(const_made, 1)
            nc.gpsimd.memset(group_of[:, 2 * H:], 0.0).then_inc(const_made, 1)
            nc.gpsimd.memset(group_of[:, 0:2 * H], 1.0).then_inc(const_made, 1)
            nc.gpsimd.memset(half_neg[:, :], -0.5).then_inc(const_made, 1)
            pool.wait_ge(const_made, 5)
            nc.gpsimd.affine_select(out=ident_f[:, :], in_=ident_f[:, :], compare_op=ALU.not_equal, fill=1.0,
                                    base=0, pattern=[[-1, 128]], channel_multiplier=1).then_inc(const_made, 1)
            nc.gpsimd.affine_select(out=ident_b[:, :], in_=ident_b[:, :], compare_op=ALU.not_equal, fill=1.0,
                                    base=0, pattern=[[-1, 128]], channel_multiplier=1).then_inc(const_made, 1)
            nc.gpsimd.affine_select(out=group_of[:, 0:2 * H], in_=group_of[:, 0:2 * H], compare_op=ALU.is_ge,
                                    fill=0.0, base=0, pattern=[[-D, 2 * H]], channel_multiplier=1)\
              .then_inc(const_made, 1)
            pool.wait_ge(const_made, 8)
            nc.gpsimd.affine_select(out=group_of[:, 0:2 * H], in_=group_of[:, 0:2 * H], compare_op=ALU.is_ge,
                                    fill=0.0, base=D - 1, pattern=[[D, 2 * H]], channel_multiplier=-1)\
              .then_inc(const_made, 1)

            def feed(b, c, m, s):
                u = U(b, c, m)
                wait(pool, unit_done, u - RING + 1)
                nc.gpsimd.tensor_copy(ring_f[:, s, :, :].rearrange("p h o -> p (h o)"),
                                      feats_f[:, ds((b % 2) * (TILES * H * OC) + (H * OC) * m, H * OC)])\
                  .then_inc(ring_ready, 1)

            def feeds(b, c, g, places=range(RING)):
                for s in places:
                    feed(b, c, g * RING + s, s)

            def head(b, c, first=False, last=False):
                if c == 0:
                    wait(pool, prep_read, FEAT(b, 1) + 1)
                feeds(b, c, 0, range(RING - 1))
                if c and not last:
                    split(pool, b + 1, 2 * (c - 1))
                feeds(b, c, 0, (RING - 1,))
                if not (last and c >= 1):
                    load_adj(K(b, c) + 2)
                if c == 0 and not first:
                    finish(pool, b - 1, CHUNKS - 1)

            def batch(b, last=False):
                if not last:
                    norm_centre(pool, b + 1)
                feeds(b, 0, 1)
                if not last:
                    norm_rstd(b + 1)
                    norm_scale(pool, b + 1)
                feeds(b, 0, 2)
                for c in range(1, CHUNKS):
                    head(b, c, last=last)
                    feeds(b, c, 1, range(2))
                    if c == 1 and not last:
                        split(pool, b + 1, 1)
                    feeds(b, c, 1, range(2, RING))
                    feeds(b, c, 2)
                    finish(pool, b, c - 1)

            pool.wait_ge(const_made, 9)
            pool.wait_ge(const_loaded, 64)
            pool.wait_ge(x_loaded, 16)
            norm_rstd(0)
            load_adj(1)
            head(0, 0, first=True)
            with pool.Fori(0, B - 1) as b:
                batch(b)
                head(b + 1, 0)
            batch(B - 1, last=True)

            with by_flag(pool):
                all_stored(pool)
                with pool.Fori(0, B) as b:
                    wait(pool, g_ln, 7 * b + 6)
                    nc.gpsimd.tensor_tensor(rstd[:, :], var_e[:, :], half_neg[:, :], ALU.pow).then_inc(g_rstd, 1)

        @block.scalar
        def _(act):
            def read_hT(b, k):
                wait(act, prep_made, HT(b, k) + 1)
                nc.scalar.activation(hT[:, CN * k:CN * k + CN], prep_ps[0:F, 0:CN], ACT.Relu).then_inc(prep_read, 1)

            def read_proj(b, k):
                cols = slice(CN * k, CN * k + CN)
                wait(act, prep_made, PROJ(b, k) + 1)
                wait(act, split_g, 12 * b)
                nc.scalar.activation(proj_sq[:, cols], prep_ps[:, 0:CN], ACT.Square)
                nc.scalar.activation(proj[:, cols], prep_ps[:, 0:CN], ACT.Copy).then_inc(prep_read, 1)

            def read_feats(b, k, first=False):
                half = TILES // 2
                wait(act, prep_made, FEAT(b, k) + 1)
                if not first:
                    wait(act, ring_ready, U(b - 1, 0, 0) + 1)
                if first:
                    act.wait_ge(zero_made, 3)
                dst = feats_f[:, ds((b % 2) * (TILES * H * OC) + k * half * H * OC, half * H * OC)]\
                    .rearrange("p (t o) -> p t o", o=OC)[:, :, 0:D]
                nc.scalar.activation(dst, prep_ps[0:P, 0:half * F].rearrange("p (t o) -> p t o", o=D), ACT.Copy)\
                  .then_inc(prep_read, 1)

            def read_prep(b, step, first=False):
                if step < 6 and step % 2 == 0:
                    read_hT(b, step // 2)
                elif step < 6:
                    read_proj(b, step // 2)
                else:
                    read_feats(b, step - 6, first)

            def read_b(b, c, m, s):
                u = U(b, c, m)
                wait(act, b_ready, u + 1)
                wait(act, unit_done, u - RING + 1)
                nc.scalar.activation(work[:, s, 1:H, :], banks_b[:, :, 0:CN], ACT.Copy).then_inc(b_out, 1)

            def exps(u, s):
                wait(act, leaky, u + 1)
                nc.scalar.activation(work[:, s, :, :], work[:, s, :, :], ACT.Exp, scale=0.25).then_inc(probs, 1)

            def read_acc(k):
                wait(act, unit_done, TILES * (k + 1))
                nc.scalar.activation(acc_sb[:, :], acc_ps[:, 0:CN], ACT.Copy).then_inc(acc_read, 1)

            def head(b, c, first=False, last=False):
                for s in range(RING):
                    if s == RING - 1 and not first:
                        read_acc(K(b, c) - 1)
                    read_b(b, c, s, s)
                    if s in ACT_MASKS and not (last and c == CHUNKS - 1):
                        read_mask(act, U(b, c, s) + TILES, K(b, c) + 1, s)
                    if c and not last:
                        read_prep(b + 1, RING * (c - 1) + s)
                    if not (first and s < 2):
                        exps(U(b, c, s) - 2, (s - 2) % RING)

            def steady(b, c, last_chunk=False):
                with act.Fori(1, GROUPS) as g:
                    for s in range(RING):
                        m = g * RING + s
                        read_b(b, c, m, s)
                        if s in ACT_MASKS and not last_chunk:
                            read_mask(act, U(b, c, m) + TILES, K(b, c) + 1, m)
                        exps(U(b, c, m) - 2, (s - 2) % RING)

            def batch(b, last=False):
                steady(b, 0)
                for c in range(1, CHUNKS):
                    head(b, c, last=last)
                    steady(b, c, last_chunk=last and c == CHUNKS - 1)

            for m in range(EARLY):
                read_mask(act, m, 0, m)
            for step in range(8):
                read_prep(0, step, first=True)
                read_mask(act, EARLY + step, 0, EARLY + step)
            head(0, 0, first=True)
            with act.Fori(0, B - 1) as b:
                batch(b)
                head(b + 1, 0)
            batch(B - 1, last=True)
            exps(U(B, 0, 0) - 2, RING - 2)
            exps(U(B, 0, 0) - 1, RING - 1)
            read_acc(B * CHUNKS - 1)

            with by_flag(act):
                all_stored(act)
                with act.Fori(0, B) as b:
                    for k in range(3):
                        wait(act, g_prep, 11 * b + k + 1)
                        nc.scalar.activation(hT[:, CN * k:CN * k + CN], prep_ps[0:F, 0:CN], ACT.Relu).then_inc(g_read, 1)
                    for n, to in enumerate((g_self, g_other)):
                        for k in range(3):
                            wait(act, g_prep, 11 * b + 3 * n + k + 4)
                            nc.scalar.activation(to[:, CN * k:CN * k + CN], prep_ps[0:F, 0:CN], ACT.Copy)\
                              .then_inc(g_read, 1)
                    for k in range(2):
                        wait(act, g_prep, 11 * b + k + 10)
                        half = TILES // 2
                        nc.scalar.activation(
                            g_feats[:, half * k:half * k + half, :, 0:D].rearrange("p m h o -> p (m h) o"),
                            prep_ps[0:P, 0:half * F].rearrange("p (t o) -> p t o", o=D), ACT.Copy).then_inc(g_read, 1)
                    with act.Fori(0, TILES) as i:
                        for h in range(H):
                            t = T(b, i)
                            q = H * t + h
                            wait(act, g_v, VS(t, h, "negate"))
                            nc.scalar.activation(g_prob, g_prob, ACT.Exp, bias=neg_max[:, :],
                                                 accum_out=row_sum[:, :]).then_inc(g_exp, 1)
                            wait(act, g_turn, q + 1)
                            nc.scalar.activation(g_turned.rearrange("p (a n) -> p a n", a=3), g_banks, ACT.Copy)\
                              .then_inc(g_copied, 1)

        @block.vector
        def _(dve):
            nc.vector.memset(zeros[:, :], 0.0).then_inc(zero_made, 1)
            nc.vector.memset(feats_f[:, :], 1.0).then_inc(zero_made, 1)
            nc.vector.memset(norms[:, :], 0.0).then_inc(zero_made, 1)

            def norm_sum(b):
                if isinstance(b, int) and b == 0:
                    dve.wait_ge(x_loaded, 16)
                else:
                    dve.wait_ge(x_loaded, 16 * B)
                wait(dve, ln_g, 4 * b)
                xb = x_sb[:, :, :, :].rearrange("p b i f -> p (b i f)")[:, ds(b * (TILES * F), TILES * F)]\
                    .rearrange("p (i f) -> p i f", i=TILES)
                nc.vector.tensor_reduce(sums[:, :], xb, AX.X, ALU.add).then_inc(ln_v, 1)
                wait(dve, ln_v, 4 * b + 1)
                nc.vector.tensor_scalar(mean[:, :], sums[:, :], 1.0 / F, None, ALU.mult).then_inc(ln_v, 1)

            def norm_var(b):
                wait(dve, ln_g, 4 * b + 2)
                nc.vector.tensor_reduce(var_s[:, :], squared[:, :, :], AX.X, ALU.add).then_inc(ln_v, 1)
                wait(dve, ln_v, 4 * b + 3)
                nc.vector.tensor_scalar(var_e[:, :], var_s[:, :], 1.0 / F, EPS, ALU.mult, ALU.add).then_inc(ln_v, 1)

            def unit(b, c, m, s, last_chunk=False):
                u, k = U(b, c, m), K(b, c)
                wait(dve, a_ready, u + 1)
                wait(dve, unit_done, u - RING + 1)
                wait(dve, tr_read, u + 1)
                mask = maskT_f[:, ds((k % 2) * (TILES * CN) + CN * m, CN)]
                nc.vector.tensor_tensor(work[:, s, 0, :], bank_a[:, 0:CN], mask, ALU.add).then_inc(a_out, 1)
                if s not in ACT_MASKS and not last_chunk:
                    read_mask(dve, u + TILES, k + 1, m)

            def leak(u, s):
                wait(dve, a_out, u + 1)
                wait(dve, b_out, u + 1)
                w = work[:, s, :, :].rearrange("p h n -> p (h n)")
                nc.vector.scalar_tensor_tensor(w, w, SLOPE, w, ALU.mult, ALU.max).then_inc(leaky, 1)

            def chunk_end(b, c):
                n = 3 * K(b, c)
                o = o_ps[:, :, :].rearrange("p j (h r) -> p j h r", h=H)
                wait(dve, o_made, K(b, c) + 1)
                wait(dve, stored, 16 * (K(b, c) + 1))
                nc.vector.tensor_scalar(den[:, :, :], o[:, :, :, D], TINY, None, ALU.max).then_inc(o_v, 1)
                wait(dve, o_v, n + 1)
                nc.vector.reciprocal(rec[:, :, :], den[:, :, :]).then_inc(o_v, 1)
                wait(dve, o_v, n + 2)
                nc.vector.tensor_tensor(res[:, :, :, :], o[:, :, :, 0:D],
                                        rec[:, :, :].unsqueeze(3).to_broadcast([P, JT, H, D]), ALU.mult)\
                  .then_inc(o_v, 1)

            def read_norm(b):
                wait(dve, prep_made, NORM(b) + 1)
                nc.vector.tensor_reduce(norms[:, ds(b, 1)], prep_ps[0:96, 0:CN], AX.X, ALU.max).then_inc(prep_read, 1)

            def head(b, c, first=False, last=False):
                for s in range(RING):
                    unit(b, c, s, s, last_chunk=last and c == CHUNKS - 1)
                    if not (first and s == 0):
                        leak(U(b, c, s) - 1, (s - 1) % RING)
                    if c == 0 and s == 0:
                        read_norm(b)
                if c == 0 and not first:
                    chunk_end(b - 1, CHUNKS - 1)

            def group(b, c, g, last_chunk=False):
                for s in range(RING):
                    unit(b, c, g * RING + s, s, last_chunk)
                    leak(U(b, c, g * RING + s) - 1, (s - 1) % RING)

            def steady(b, c, last_chunk=False):
                with dve.Fori(1, GROUPS) as g:
                    group(b, c, g, last_chunk)

            def batch(b, last=False):
                if not last:
                    norm_sum(b + 1)
                group(b, 0, 1)
                if not last:
                    norm_var(b + 1)
                group(b, 0, 2)
                for c in range(1, CHUNKS):
                    head(b, c, last=last)
                    steady(b, c, last_chunk=last and c == CHUNKS - 1)
                    chunk_end(b, c - 1)

            norm_sum(0)
            norm_centre(dve, 0)
            norm_var(0)
            norm_scale(dve, 0)
            for k in range(CHUNKS):
                split(dve, 0, k)
            dve.wait_ge(zero_made, 3)
            head(0, 0, first=True)
            with dve.Fori(0, B - 1) as b:
                batch(b)
                head(b + 1, 0)
            batch(B - 1, last=True)
            nc.vector.tensor_reduce(top[:, :], norms[:, :], AX.X, ALU.max).then_inc(top_v, 1)
            leak(U(B, 0, 0) - 1, RING - 1)
            dve.wait_ge(top_turned, 1)
            nc.vector.tensor_reduce(top_all[:, :], prep_ps[0:1, 0:96], AX.X, ALU.max).then_inc(top_v, 1)
            dve.wait_ge(top_v, 2)
            nc.vector.tensor_scalar(flag[:, :], top_all[:, :], SAFE, None, ALU.is_gt).then_inc(flag_made, 1)
            chunk_end(B - 1, CHUNKS - 1)
            dve.wait_ge(o_g, 3 * (B * CHUNKS - 1))
            finish(dve, B - 1, CHUNKS - 1)

            with by_flag(dve):
                all_stored(dve)
                with dve.Fori(0, B) as b:
                    n = 7 * b
                    xb = x_sb[:, :, :, :].rearrange("p b i f -> p (b i f)")[:, ds(b * (TILES * F), TILES * F)]\
                        .rearrange("p (i f) -> p i f", i=TILES)

                    def spread(stat):
                        return stat[:, :].unsqueeze(2).to_broadcast([P, TILES, F])

                    nc.vector.tensor_reduce(sums[:, :], xb, AX.X, ALU.add).then_inc(g_ln, 1)
                    wait(dve, g_ln, n + 1)
                    nc.vector.tensor_scalar(mean[:, :], sums[:, :], 1.0 / F, None, ALU.mult).then_inc(g_ln, 1)
                    wait(dve, g_ln, n + 2)
                    nc.vector.tensor_tensor(centred[:, :, :], xb, spread(mean), ALU.subtract).then_inc(g_ln, 1)
                    wait(dve, g_ln, n + 3)
                    nc.vector.tensor_tensor(squared[:, :, :], centred[:, :, :], centred[:, :, :], ALU.mult)\
                      .then_inc(g_ln, 1)
                    wait(dve, g_ln, n + 4)
                    nc.vector.tensor_reduce(var_s[:, :], squared[:, :, :], AX.X, ALU.add).then_inc(g_ln, 1)
                    wait(dve, g_ln, n + 5)
                    nc.vector.tensor_scalar(var_e[:, :], var_s[:, :], 1.0 / F, EPS, ALU.mult, ALU.add)\
                      .then_inc(g_ln, 1)
                    wait(dve, g_rstd, b + 1)
                    nc.vector.tensor_tensor(normed[:, :, :], centred[:, :, :], spread(rstd), ALU.mult)\
                      .then_inc(g_ln, 1)
                    wait(dve, g_read, 11 * b + 11)
                    dve.sem_inc(passed, 1)
                    with dve.Fori(0, TILES) as i:
                        t = T(b, i)
                        r = res[:, 0, :, :].rearrange("p h d -> p (h d)")
                        x_row = x_sb[:, :, :, :].rearrange("p b i f -> p (b i f)")[:, ds(t * F, F)]
                        wait(dve, g_loaded, 16 * (t + 1))
                        nc.vector.tensor_scalar(g_mask, g_adj, -1.0, MASKED, ALU.add, ALU.mult).then_inc(g_v, 1)
                        for h in range(H):
                            q = H * t + h

                            def done(step):
                                wait(dve, g_v, VS(t, h, step))

                            nc.vector.tensor_scalar(g_head, g_self[:, ds(P * i, P)], group_of[0:F, h:h + 1], None,
                                                    ALU.mult).then_inc(g_v, 1)
                            wait(dve, g_scores, q + 1)
                            nc.vector.tensor_tensor(g_prob.rearrange("p (a n) -> p a n", a=3), g_banks,
                                                    g_adj.rearrange("p (a n) -> p a n", a=3), ALU.mult).then_inc(g_v, 1)
                            done("adj")
                            nc.vector.scalar_tensor_tensor(g_prob, g_prob, SLOPE, g_prob, ALU.mult, ALU.max)\
                              .then_inc(g_v, 1)
                            done("leaky")
                            nc.vector.scalar_tensor_tensor(g_prob, g_prob, float(D) ** -0.5, g_mask, ALU.mult, ALU.add)\
                              .then_inc(g_v, 1)
                            done("mask")
                            nc.vector.tensor_reduce(row_max[:, :], g_prob, AX.X, ALU.max).then_inc(g_v, 1)
                            done("max")
                            nc.vector.tensor_scalar(neg_max[:, :], row_max[:, :], -1.0, None, ALU.mult).then_inc(g_v, 1)
                            wait(dve, g_exp, q + 1)
                            nc.vector.tensor_tensor(g_prob, g_prob, g_adj, ALU.mult).then_inc(g_v, 1)
                            nc.vector.reciprocal(row_rec[:, :], row_sum[:, :]).then_inc(g_v, 1)
                            done("recip")
                            wait(dve, g_out, q + 1)
                            nc.vector.tensor_scalar(res[:, 0, h, :], acc_ps[0:P, 0:D], row_rec[:, :], None, ALU.mult)\
                              .then_inc(g_v, 1)
                        end = TILE_STEPS * t + TILE_STEPS - 3
                        wait(dve, g_v, end)
                        nc.vector.tensor_tensor(r, r, bias_bc[:, :], ALU.add).then_inc(g_v, 1)
                        wait(dve, g_v, end + 1)
                        nc.vector.tensor_scalar(r, r, 0.0, None, ALU.max).then_inc(g_v, 1)
                        wait(dve, g_v, end + 2)
                        nc.vector.tensor_tensor(r, r, x_row, ALU.add).then_inc(g_v, 1)

        @block.tensor
        def _(pe):
            mm = nc.tensor.matmul

            def make_hT(b, k):
                wait(pe, prep_read, HT(b, k))
                if not isinstance(b, int):
                    pe.sem_inc(passed, 1)
                for j in range(JT):
                    ins = nc.tensor.transpose(prep_ps[0:F, P * j:P * j + P], normed[:, JT * k + j, :],
                                              ident_f[0:P, 0:P])
                ins.then_inc(prep_made, 1)

            def make_proj(b, k):
                wait(pe, prep_read, PROJ(b, k))
                mm(prep_ps[:, 0:CN], w_proj[:, :], hT[:, CN * k:CN * k + CN], start=True, stop=True)\
                    .then_inc(prep_made, 1)

            def make_feats(b, k):
                wait(pe, prep_read, FEAT(b, k))
                half = TILES // 2
                for t in range(half):
                    i = half * k + t
                    ins = mm(prep_ps[0:P, F * t:F * t + F], hT[:, P * i:P * i + P], w_f[:, :], start=True, stop=True)
                ins.then_inc(prep_made, 1)

            def make_norm(b):
                wait(pe, prep_read, NORM(b))
                for k in range(3):
                    ins = mm(prep_ps[32 * k:32 * k + 32, 0:CN], group_of[:, :], proj_sq[:, CN * k:CN * k + CN],
                             start=True, stop=True)
                ins.then_inc(prep_made, 1)

            def prep(b, step):
                if step < 6 and step % 2 == 0:
                    make_hT(b, step // 2)
                elif step < 6:
                    make_proj(b, step // 2)
                else:
                    make_feats(b, step - 6)

            def transpose_mask(t, k, m):
                wait(pe, tr_read, t)
                for j in range(JT):
                    ins = nc.tensor.transpose(tr_ps[:, j, 0:P],
                                              a_nat_f[:, ds((k % 2) * (JT * N) + j * N + P * m, P)],
                                              ident_b[0:P, 0:P])
                ins.then_inc(tr_made, 1)

            def scores(b, c, m):
                u, k = U(b, c, m), K(b, c)
                slot = (b % 2) * (H * N)
                mask = maskT_f[:, ds((k % 2) * (TILES * CN) + CN * m, CN)]

                def head_scores(h, to, stop):
                    return mm(to, other_f[:, ds(slot + h * N + P * m, P)], self_f[:, ds(slot + h * N + CN * c, CN)],
                              start=True, stop=stop)

                wait(pe, b_out, u)
                for h in range(1, H):
                    head_scores(h, banks_b[:, h - 1, 0:CN], False)
                wait(pe, tr_read, u + 1)
                for h in range(1, H):
                    ins = mm(banks_b[:, h - 1, 0:CN], ident_b[0:P, 0:P], mask, start=False, stop=True)
                ins.then_inc(b_ready, 1)
                wait(pe, a_out, u)
                head_scores(0, bank_a[:, 0:CN], True).then_inc(a_ready, 1)

            def multiply(u, s, start=False):
                wait(pe, ring_ready, u + 1)
                wait(pe, probs, u + 1)
                if start:
                    mm(acc_ps[:, 0:CN], zeros[:, 0:128], zeros[:, 0:CN], start=True, stop=True)
                for h in range(H):
                    ins = mm(acc_ps[32 * h:32 * h + OC, 0:CN], ring_f[:, s, h, :], work[:, s, h, :],
                             start=False, stop=True, skip_group_check=True)
                ins.then_inc(unit_done, 1)

            def turn_acc(k):
                wait(pe, acc_read, k + 1)
                for j in range(JT):
                    ins = nc.tensor.transpose(o_ps[:, j, :], acc_sb[:, P * j:P * j + P], ident_f[:, :])
                ins.then_inc(o_made, 1)

            def head(b, c, first=False, last=False):
                k = K(b, c)
                if c == 0:
                    wait(pe, parts_placed, PLACED if first else PLACED * (b + CHUNKS))
                for s in range(RING):
                    u = U(b, c, s)
                    if c == 1 and not last:
                        if s == 0:
                            wait(pe, ln_g, 4 * (b + 1) + 4)
                            pe.sem_inc(passed, 1)
                    scores(b, c, s)
                    if not (last and c == CHUNKS - 1):
                        if s == 0:
                            wait(pe, adj_loaded, 32 * (k + 2))
                        transpose_mask(u + TILES, k + 1, s)
                    if c == 0 and s == 0:
                        make_norm(b)
                    if c and not last:
                        prep(b + 1, RING * (c - 1) + s)
                    if s < 3:
                        if not first:
                            multiply(u - 3, (s - 3) % RING)
                    else:
                        if not first:
                            turn_acc(k - 1)
                        multiply(u - 3, 0, start=True)

            def steady(b, c, last_chunk=False):
                with pe.Fori(1, GROUPS) as g:
                    for s in range(RING):
                        m = g * RING + s
                        u = U(b, c, m)
                        scores(b, c, m)
                        if not last_chunk:
                            transpose_mask(u + TILES, K(b, c) + 1, m)
                        multiply(u - 3, (s - 3) % RING)

            def batch(b, last=False):
                steady(b, 0)
                for c in range(1, CHUNKS):
                    head(b, c, last=last)
                    steady(b, c, last_chunk=last and c == CHUNKS - 1)

            pe.wait_ge(const_made, 9)
            pe.wait_ge(adj_loaded, 32)
            for m in range(EARLY):
                transpose_mask(m, 0, m)
            pe.wait_ge(const_loaded, 64)
            pe.wait_ge(zero_made, 3)
            pe.wait_ge(ln_g, 4)
            for step in range(8):
                prep(0, step)
                transpose_mask(EARLY + step, 0, EARLY + step)
            head(0, 0, first=True)
            pe.wait_ge(parts_placed, PLACED * CHUNKS)
            with pe.Fori(0, B - 1) as b:
                batch(b)
                head(b + 1, 0)
            batch(B - 1, last=True)
            pe.wait_ge(top_v, 1)
            mm(prep_ps[0:1, 0:96], top[:, :], ident_f[0:96, 0:96], start=True, stop=True).then_inc(top_turned, 1)
            for s in range(1, RING):
                multiply(U(B, 0, 0) - RING + s, s)
            turn_acc(B * CHUNKS - 1)

            with by_flag(pe):
                all_stored(pe)
                def free(n):
                    wait(pe, g_read, n)
                    pe.sem_inc(passed, 1)

                with pe.Fori(0, B) as b:
                    wait(pe, g_ln, 7 * b + 7)
                    pe.sem_inc(passed, 1)
                    for k in range(3):
                        if k:
                            free(11 * b + k)
                        for j in range(JT):
                            ins = nc.tensor.transpose(prep_ps[0:F, P * j:P * j + P], normed[:, JT * k + j, :],
                                                      ident_f[0:P, 0:P])
                        ins.then_inc(g_prep, 1)
                    for n in range(2):
                        for k in range(3):
                            free(11 * b + 3 * n + k + 3)
                            mm(prep_ps[0:F, 0:CN], w_proj[:, F * n:F * n + F], hT[:, CN * k:CN * k + CN],
                               start=True, stop=True).then_inc(g_prep, 1)
                    for k in range(2):
                        free(11 * b + k + 9)
                        half = TILES // 2
                        for j in range(half):
                            i = half * k + j
                            ins = mm(prep_ps[0:P, F * j:F * j + F], hT[:, P * i:P * i + P], w_f[:, :],
                                     start=True, stop=True)
                        ins.then_inc(g_prep, 1)
                    with pe.Fori(0, TILES) as i:
                        t = T(b, i)
                        for h in range(H):
                            q = H * t + h
                            wait(pe, g_v, VS(t, h, "select"))
                            for n in range(3):
                                ins = mm(g_banks[:, n, :], g_head, g_other[:, CN * n:CN * n + CN], start=True, stop=True)
                            ins.then_inc(g_scores, 1)
                            wait(pe, g_v, VS(t, h, "keep"))
                            for m in range(TILES):
                                ins = nc.tensor.transpose(g_banks[:, m // JT, P * (m % JT):P * (m % JT) + P],
                                                          g_prob[:, P * m:P * m + P], ident_f[0:P, 0:P])
                            ins.then_inc(g_turn, 1)
                            wait(pe, g_copied, q + 1)
                            for m in range(TILES):
                                ins = mm(acc_ps[0:P, 0:D], g_turned[:, P * m:P * m + P], g_feats[:, m, h, 0:D],
                                         start=m == 0, stop=m == TILES - 1)
                            ins.then_inc(g_out, 1)


_INS = ["x", "adj", "L0_gnn_kernel", "L0_gnn_attention_kernel", "L0_gnn_attention_kernel_2", "L0_gnn_bias"]


def kernel(**inputs):
    import concourse.bacc as bacc
    from concourse import mybir
    from concourse.bass_utils import run_bass_kernel_spmd as run

    nc = bacc.Bacc("TRN2", target_bir_lowering=False, num_devices=1)
    arrays, args = {}, []
    for name in _INS:
        a = np.ascontiguousarray(inputs[name])
        arrays[name] = a
        args.append(nc.dram_tensor(name, a.shape, mybir.dt.from_np(a.dtype), kind="ExternalInput").ap())
    args.append(nc.dram_tensor("out", (B, N, H * D), mybir.dt.float32, kind="ExternalOutput").ap())
    gat_program(nc, *args)
    r = run(nc, [arrays], core_ids=[0])
    return r.results[0]["out"]
```

```python
import numpy as np

B, N, F = 8, 1500, 64
H, D = 4, 16
P = 125
TILES = N // P
CHUNKS = 3
JT = TILES // CHUNKS
CN = JT * P
RING = 4
GROUPS = TILES // RING
UNITS = CHUNKS * TILES
PARTS = 6
KS = PARTS * D
SELF_PART = (0, 0, 0, 1, 1, 2)
OTHER_PART = (0, 1, 2, 0, 1, 0)
OC = D + 1
SLOPE = 0.2
EPS = 1e-5
BIG = float(2 ** 20)
TINY = 1e-30
SAFE = 192.0
BANK = 512
HEAD_STEPS = ("select", "adj", "leaky", "mask", "max", "negate", "keep", "recip", "scale")
TILE_STEPS = 1 + H * len(HEAD_STEPS) + 3
PLACED = 16 * 2 * PARTS
MASKED = 1e9
TWO_HEADS = 1


def gat_program(nc, x, adj, w_feat, w_self, w_other, bias, out):
    import concourse.bass as bass
    from concourse import mybir
    from contextlib import ExitStack

    f32, bf16, i32 = mybir.dt.float32, mybir.dt.bfloat16, mybir.dt.int32
    ALU, ACT, AX = mybir.AluOpType, mybir.ActivationFunctionType, mybir.AxisListType
    ds = bass.ds

    part_d = nc.dram_tensor("part_scratch", (2, H, D, 3, N), bf16, kind="Internal").ap()

    x_v = x.rearrange("b (i p) f -> b p i f", p=P)
    adj_v = adj.rearrange("b (c j p) m -> (b c) p j m", c=CHUNKS, j=JT)
    out_v = out.rearrange("b (c j p) f -> (b c) p j f", c=CHUNKS, j=JT)

    ctx = ExitStack()
    with ctx:
        def sb(name, shape, dt):
            return ctx.enter_context(nc.sbuf_tensor(name, shape, dt))

        def pb(name, shape, dt):
            return ctx.enter_context(nc.psum_tensor(name, shape, dt))

        def sem(name):
            return ctx.enter_context(nc.semaphore(name))

        w_proj = sb("w_proj", [F, 2 * H * D], f32)
        w_f = sb("w_f", [F, H * D], f32)
        bias_bc = sb("bias_bc", [P, H * D], f32)
        ident_f = sb("ident_f", [128, 128], f32)
        edge_or_big = sb("edge_or_big", [P + 1, P], bf16)
        ones = sb("ones", [1, CN], bf16)
        zeros = sb("zeros", [P, BANK], bf16)
        group_of = sb("group_of", [128, 32], bf16)
        half_neg = sb("half_neg", [P, TILES], f32)
        x_sb = sb("x_sb", [P, B, TILES, F], f32)
        sums = sb("sums", [P, TILES], f32)
        mean = sb("mean", [P, TILES], f32)
        var_s = sb("var_s", [P, TILES], f32)
        var_e = sb("var_e", [P, TILES], f32)
        rstd = sb("rstd", [P, TILES], f32)
        centred = sb("centred", [P, TILES, F], f32)
        squared = sb("squared", [P, TILES, F], f32)
        normed = sb("normed", [P, TILES, F], f32)
        hT = sb("hT", [F, N], f32)
        proj = sb("proj", [128, N], f32)
        proj_sq = sb("proj_sq", [128, N], bf16)
        part = sb("part", [128, 3, N], bf16)
        rest = sb("rest", [128, CN], f32)
        self_k = sb("self_k", [KS, 2, H, N], bf16)
        other_k = sb("other_k", [KS, 2, H, N], bf16)
        feats = sb("feats", [P, 2, TILES, H * OC], f32)
        norms = sb("norms", [96, B], f32)
        a_nat = sb("a_nat", [P + 1, 2, JT, N], bf16)
        work = sb("work", [P, RING, H, CN], f32)
        ring_f = sb("ring_f", [P, RING, H, OC], f32)
        acc_sb = sb("acc_sb", [128, CN], f32)
        den = sb("den", [P, JT, H], f32)
        rec = sb("rec", [P, JT, H], f32)
        res = sb("res", [P, JT, H, D], f32)

        score_ps = pb("score_ps", [P, 2 + H, BANK], f32)
        acc_ps = pb("acc_ps", [128, BANK], f32)
        prep_ps = pb("prep_ps", [128, BANK], f32)
        o_ps = score_ps[:, 2, :].rearrange("p (j c) -> p j c", j=JT)

        flag = sb("flag", [1, 1], i32)
        top = sb("top", [96, 1], f32)
        top_all = sb("top_all", [1, 1], f32)
        row_max = sb("row_max", [P, 1], f32)
        neg_max = sb("neg_max", [P, 1], f32)
        row_sum = sb("row_sum", [P, 1], f32)
        row_rec = sb("row_rec", [P, 1], f32)
        work_f = work[:, :, :, :].rearrange("p s h n -> p (s h n)")
        g_prob = work_f[:, 0:N]
        g_adj = work_f[:, N:2 * N]
        g_mask = work_f[:, 2 * N:3 * N]
        g_turned = work_f[:, 3 * N:4 * N]
        g_self = proj[0:F, :]
        g_other = self_k[0:F, :, :, :].rearrange("k s h n -> k (s h n)").bitcast(f32)[:, 0:N]
        g_head = self_k[0:F, :, :, :].rearrange("k s h n -> k (s h n)").bitcast(f32)[:, N:N + P]
        g_feats = feats[:, 0, :, :].rearrange("p m (h o) -> p m h o", h=H)
        g_banks = score_ps[:, 3:6, 0:CN]

        self_f = self_k[:, :, :, :].rearrange("k s h n -> k (s h n)")
        other_f = other_k[:, :, :, :].rearrange("k s h n -> k (s h n)")
        a_nat_f = a_nat[:, :, :, :].rearrange("p s j n -> p (s j n)")
        feats_f = feats[:, :, :, :].rearrange("p s m c -> p (s m c)")

        const_loaded = sem("const_loaded")
        x_loaded = sem("x_loaded")
        const_made = sem("const_made")
        zero_made = sem("zero_made")
        adj_loaded = sem("adj_loaded")
        ln_v = sem("ln_v")
        ln_g = sem("ln_g")
        prep_made = sem("prep_made")
        prep_read = sem("prep_read")
        squared_g = sem("squared_g")
        split_g = sem("split_g")
        parts_out = sem("parts_out")
        parts_placed = sem("parts_placed")
        ones_made = sem("ones_made")
        ones_placed = sem("ones_placed")
        a_ready = sem("a_ready")
        b_ready = sem("b_ready")
        a_out = sem("a_out")
        b_out = sem("b_out")
        leaky = sem("leaky")
        probs = sem("probs")
        ring_ready = sem("ring_ready")
        unit_done = sem("unit_done")
        acc_read = sem("acc_read")
        o_made = sem("o_made")
        o_v = sem("o_v")
        o_g = sem("o_g")
        stored = sem("stored")

        top_v = sem("top_v")
        top_turned = sem("top_turned")
        flag_made = sem("flag_made")
        g_ln = sem("g_ln")
        g_rstd = sem("g_rstd")
        g_prep = sem("g_prep")
        g_read = sem("g_read")
        g_loaded = sem("g_loaded")
        g_v = sem("g_v")
        g_scores = sem("g_scores")
        g_exp = sem("g_exp")
        g_turn = sem("g_turn")
        g_copied = sem("g_copied")
        g_out = sem("g_out")
        g_stored = sem("g_stored")
        passed = sem("passed")

        block = ctx.enter_context(nc.Block())

        def U(b, c, m):
            return UNITS * b + TILES * c + m

        def K(b, c):
            return CHUNKS * b + c

        def HT(b, k):
            return 9 * b + 2 * k

        def PROJ(b, k):
            return 9 * b + 2 * k + 1

        def FEAT(b, k):
            return 9 * b + 6 + k

        def NORM(b):
            return 9 * b + 8

        def wait(eng, s, value):
            if isinstance(value, int) and value <= 0:
                return
            eng.wait_ge(s, value)
            if not isinstance(value, int) and (eng is nc.gpsimd or eng is nc.sync):
                eng.sem_inc(passed, 1)

        def heads_of_dve(s):
            return 2 if s == TWO_HEADS else 1

        def by_flag(eng):
            eng.wait_ge(flag_made, 1)
            return eng.If(eng.value_load(flag[0:1, 0:1], min_val=0, max_val=1) == 1)

        def all_stored(eng):
            eng.wait_ge(stored, 16 * (B * CHUNKS + 1))

        def T(b, i):
            return TILES * b + i

        def VS(t, h, step):
            return TILE_STEPS * t + 1 + len(HEAD_STEPS) * h + HEAD_STEPS.index(step) + 1

        def read_hT(eng, b, k):
            wait(eng, prep_made, HT(b, k) + 1)
            to, fr = hT[:, CN * k:CN * k + CN], prep_ps[0:F, 0:CN]
            if eng is nc.vector:
                ins = nc.vector.tensor_scalar(to, fr, 0.0, None, ALU.max)
            else:
                ins = nc.scalar.activation(to, fr, ACT.Relu)
            ins.then_inc(prep_read, 1)

        def norm_centre(eng, b):
            xb = x_sb[:, :, :, :].rearrange("p b i f -> p (b i f)")[:, ds(b * (TILES * F), TILES * F)]\
                .rearrange("p (i f) -> p i f", i=TILES)
            wait(eng, ln_v, 4 * b + 2)
            wait(eng, prep_made, HT(b - 1, 2) + 1)
            eng.tensor_tensor(centred[:, :, :], xb, mean[:, :].unsqueeze(2).to_broadcast([P, TILES, F]),
                              ALU.subtract).then_inc(ln_g, 1)
            wait(eng, ln_g, 4 * b + 1)
            eng.tensor_tensor(squared[:, :, :], centred[:, :, :], centred[:, :, :], ALU.mult).then_inc(ln_g, 1)

        def norm_rstd(b):
            wait(nc.gpsimd, ln_v, 4 * b + 4)
            nc.gpsimd.tensor_tensor(rstd[:, :], var_e[:, :], half_neg[:, :], ALU.pow).then_inc(ln_g, 1)

        def norm_scale(eng, b):
            wait(eng, ln_g, 4 * b + 3)
            eng.tensor_tensor(normed[:, :, :], centred[:, :, :],
                              rstd[:, :].unsqueeze(2).to_broadcast([P, TILES, F]), ALU.mult).then_inc(ln_g, 1)

        def split(eng, b, k):
            cols = slice(CN * k, CN * k + CN)
            if k == 0 and not isinstance(b, int):
                wait(eng, parts_out, 16 * (b - 1 + CHUNKS))
            wait(eng, prep_read, PROJ(b, k) + 1)
            n = 12 * b + 4 * k
            eng.tensor_copy(part[:, 0, cols], proj[:, cols]).then_inc(split_g, 1)
            wait(eng, split_g, n + 1)
            eng.tensor_tensor(rest[:, :], proj[:, cols], part[:, 0, cols], ALU.subtract).then_inc(split_g, 1)
            wait(eng, split_g, n + 2)
            eng.tensor_copy(part[:, 1, cols], rest[:, :]).then_inc(split_g, 1)
            wait(eng, split_g, n + 3)
            eng.tensor_tensor(part[:, 2, cols], rest[:, :], part[:, 1, cols], ALU.subtract).then_inc(split_g, 1)
            eng.tensor_tensor(proj_sq[:, cols], proj[:, cols], proj[:, cols], ALU.mult).then_inc(squared_g, 1)

        def finish(eng, b, c):
            n = 3 * K(b, c)
            xc = x_sb[:, :, :, :].rearrange("p b i f -> p (b i f)")[:, ds(K(b, c) * (JT * F), JT * F)]
            r = res[:, :, :, :].rearrange("p j h d -> p j (h d)")
            rf = res[:, :, :, :].rearrange("p j h d -> p (j h d)")
            wait(eng, o_v, n + 6)
            eng.tensor_tensor(r, r, bias_bc[:, :].unsqueeze(1).to_broadcast([P, JT, H * D]), ALU.add)\
              .then_inc(o_g, 1)
            wait(eng, o_g, n + 1)
            eng.tensor_scalar(rf, rf, 0.0, None, ALU.max).then_inc(o_g, 1)
            wait(eng, o_g, n + 2)
            eng.tensor_tensor(rf, rf, xc, ALU.add).then_inc(o_g, 1)

        @block.sync
        def _(sp):
            sp.dma_start(x_sb[:, 0, :, :], x_v[0]).then_inc(x_loaded, 16)
            sp.dma_start(w_proj[:, 0:H * D].rearrange("f (h d) -> f h d", h=H),
                         w_self.rearrange("h f d -> f h d")).then_inc(const_loaded, 16)
            sp.dma_start(w_proj[:, H * D:].rearrange("f (h d) -> f h d", h=H),
                         w_other.rearrange("h f d -> f h d")).then_inc(const_loaded, 16)
            sp.dma_start(w_f[:, :].rearrange("f (h d) -> f h d", h=H),
                         w_feat.rearrange("h f d -> f h d")).then_inc(const_loaded, 16)
            sp.dma_start(bias_bc[:, :], bias.rearrange("a b h d -> (a b) (h d)").to_broadcast([P, H * D]))\
              .then_inc(const_loaded, 16)
            sp.wait_ge(ones_made, 1)
            sp.dma_start(a_nat_f[P:P + 1, :].rearrange("p (r n) -> p r n", n=CN),
                         ones[:, :].unsqueeze(1).to_broadcast([1, 2 * JT * N // CN, CN])).then_inc(ones_placed, 16)
            sp.wait_ge(x_loaded, 16)
            sp.dma_start(x_sb[:, 1, :, :], x_v[1]).then_inc(x_loaded, 16)

            def part_out(b, k=None):
                cols = slice(0, N) if k is None else slice(CN * k, CN * k + CN)
                wait(sp, split_g, 12 * (b + 1) if k is None else 4 * (k + 1))
                sp.dma_start(part_d.rearrange("s h d w n -> (s h d) w n")[:, :, cols], part[:, :, cols])\
                  .then_inc(parts_out, 16)

            def place(b, k=None):
                cols = slice(0, N) if k is None else slice(CN * k, CN * k + CN)
                wait(sp, parts_out, 16 * (b + CHUNKS if k is None else k + 1))
                if k is None:
                    wait(sp, b_ready, U(b - 1, 0, 0) + 1)
                for n in range(PARTS):
                    for side, dst, which in ((0, self_f, SELF_PART), (1, other_f, OTHER_PART)):
                        sp.dma_start(
                            dst[D * n:D * n + D, ds((b % 2) * (H * N), H * N)]
                            .rearrange("d (h n) -> d h n", h=H)[:, :, cols],
                            part_d[side, :, :, which[n], cols].rearrange("h d n -> d h n")).then_inc(parts_placed, 16)

            def store(b, c):
                wait(sp, o_g, 3 * (K(b, c) + 1))
                k = K(b, c)
                sp.dma_start(out_v[ds(k, 1)].rearrange("o p j f -> (o p) j f"),
                             res[:, :, :, :].rearrange("p j h d -> p j (h d)")).then_inc(stored, 16)

            sp.sem_inc(stored, 16)
            part_out(0, 0)
            place(0, 0)
            part_out(0, 1)
            place(0, 1)
            part_out(0, 2)
            place(0, 2)
            for b in range(2, B):
                sp.wait_ge(x_loaded, 16 * b)
                sp.dma_start(x_sb[:, b, :, :], x_v[b]).then_inc(x_loaded, 16)
            with sp.Fori(0, B - 1) as b:
                store(b, 0)
                part_out(b + 1)
                place(b + 1)
                store(b, 1)
                store(b, 2)
            for c in range(CHUNKS):
                store(B - 1, c)
            sp.wait_ge(stored, 16 * (B * CHUNKS + 1))

            with by_flag(sp):
                rows = adj.rearrange("b (i p) m -> (b i) p m", p=P)
                outs = out.rearrange("b (i p) f -> (b i) p f", p=P)

                def load(t):
                    sp.dma_start(g_adj.rearrange("p (o n) -> p o n", o=1), rows[ds(t, 1)].rearrange("o p n -> p o n"))\
                      .then_inc(g_loaded, 16)

                load(0)
                with sp.Fori(0, B * TILES - 1) as t:
                    wait(sp, g_v, TILE_STEPS * (t + 1))
                    sp.dma_start(outs[ds(t, 1)].rearrange("o p f -> (o p) f"),
                                 res[:, 0, :, :].rearrange("p h d -> p (h d)")).then_inc(g_stored, 16)
                    wait(sp, g_stored, 16 * (t + 1))
                    load(t + 1)
                sp.wait_ge(g_v, TILE_STEPS * B * TILES)
                sp.dma_start(outs[B * TILES - 1], res[:, 0, :, :].rearrange("p h d -> p (h d)")).then_inc(g_stored, 16)
                sp.wait_ge(g_stored, 16 * B * TILES)

        @block.gpsimd
        def _(pool):
            def load_adj(k):
                wait(pool, adj_loaded, 32 * k)
                wait(pool, b_ready, TILES * (k - 1))
                for rows in (slice(0, 112), slice(112, P)):
                    pool.dma_start(
                        a_nat_f[rows, ds((k % 2) * (JT * N), JT * N)].rearrange("p (o j n) -> p o j n", o=1, j=JT),
                        adj_v[ds(k, 1)].rearrange("o p j n -> p o j n")[rows]).then_inc(adj_loaded, 16)

            load_adj(0)
            nc.gpsimd.memset(ones[:, :], 1.0).then_inc(ones_made, 1)
            nc.gpsimd.memset(ident_f[:, :], 0.0).then_inc(const_made, 1)
            nc.gpsimd.memset(edge_or_big[:, :], 0.0).then_inc(const_made, 1)
            nc.gpsimd.memset(group_of[:, 2 * H:], 0.0).then_inc(const_made, 1)
            nc.gpsimd.memset(group_of[:, 0:2 * H], 1.0).then_inc(const_made, 1)
            nc.gpsimd.memset(half_neg[:, :], -0.5).then_inc(const_made, 1)
            pool.wait_ge(const_made, 5)
            nc.gpsimd.affine_select(out=ident_f[:, :], in_=ident_f[:, :], compare_op=ALU.not_equal, fill=1.0,
                                    base=0, pattern=[[-1, 128]], channel_multiplier=1).then_inc(const_made, 1)
            nc.gpsimd.affine_select(out=edge_or_big[:, :], in_=edge_or_big[:, :], compare_op=ALU.not_equal, fill=BIG,
                                    base=0, pattern=[[-1, P]], channel_multiplier=1).then_inc(const_made, 1)
            nc.gpsimd.affine_select(out=group_of[:, 0:2 * H], in_=group_of[:, 0:2 * H], compare_op=ALU.is_ge,
                                    fill=0.0, base=0, pattern=[[-D, 2 * H]], channel_multiplier=1)\
              .then_inc(const_made, 1)
            pool.wait_ge(const_made, 8)
            nc.gpsimd.affine_select(out=group_of[:, 0:2 * H], in_=group_of[:, 0:2 * H], compare_op=ALU.is_ge,
                                    fill=0.0, base=D - 1, pattern=[[D, 2 * H]], channel_multiplier=-1)\
              .then_inc(const_made, 1)
            nc.gpsimd.affine_select(out=edge_or_big[:, :], in_=edge_or_big[:, :], compare_op=ALU.is_ge, fill=-BIG,
                                    base=P - 1, pattern=[[0, P]], channel_multiplier=-1).then_inc(const_made, 1)

            def feed(b, c, m, s):
                u = U(b, c, m)
                wait(pool, unit_done, u - RING + 1)
                nc.gpsimd.tensor_copy(ring_f[:, s, :, :].rearrange("p h o -> p (h o)"),
                                      feats_f[:, ds((b % 2) * (TILES * H * OC) + (H * OC) * m, H * OC)])\
                  .then_inc(ring_ready, 1)

            def feeds(b, c, g, places=range(RING)):
                for s in places:
                    feed(b, c, g * RING + s, s)

            def head(b, c, first=False, last=False):
                if not (last and c == CHUNKS - 1):
                    load_adj(K(b, c) + 1)
                if c == 0:
                    wait(pool, prep_read, FEAT(b, 0) + 1)
                feeds(b, c, 0, range(RING - 1))
                if c and not last:
                    split(pool, b + 1, c - 1)
                feeds(b, c, 0, (RING - 1,))
                if c == 0 and not first:
                    finish(pool, b - 1, CHUNKS - 1)

            def batch(b, last=False):
                if not last:
                    norm_centre(pool, b + 1)
                wait(pool, prep_read, FEAT(b, 1) + 1)
                feeds(b, 0, 1)
                if not last:
                    norm_rstd(b + 1)
                    norm_scale(pool, b + 1)
                feeds(b, 0, 2)
                for c in range(1, CHUNKS):
                    head(b, c, last=last)
                    feeds(b, c, 1, (0,))
                    if c == 2 and not last:
                        split(pool, b + 1, 2)
                    feeds(b, c, 1, range(1, RING))
                    feeds(b, c, 2)
                    finish(pool, b, c - 1)

            pool.wait_ge(const_made, 10)
            pool.wait_ge(const_loaded, 64)
            pool.wait_ge(x_loaded, 16)
            norm_rstd(0)
            head(0, 0, first=True)
            with pool.Fori(0, B - 1) as b:
                batch(b)
                head(b + 1, 0)
            batch(B - 1, last=True)

            with by_flag(pool):
                all_stored(pool)
                with pool.Fori(0, B) as b:
                    wait(pool, g_ln, 7 * b + 6)
                    nc.gpsimd.tensor_tensor(rstd[:, :], var_e[:, :], half_neg[:, :], ALU.pow).then_inc(g_rstd, 1)

        @block.scalar
        def _(act):
            def read_proj(b, k):
                cols = slice(CN * k, CN * k + CN)
                wait(act, prep_made, PROJ(b, k) + 1)
                wait(act, squared_g, CHUNKS * b)
                nc.scalar.activation(proj[:, cols], prep_ps[:, 0:CN], ACT.Copy).then_inc(prep_read, 1)

            def read_b(b, c, m, s):
                u = U(b, c, m)
                n = heads_of_dve(s)
                wait(act, b_ready, u + 1)
                wait(act, unit_done, u - RING + 1)
                nc.scalar.activation(work[:, s, n:H, :], score_ps[:, 2 + n:, 0:CN], ACT.Copy).then_inc(b_out, 1)

            def exps(u, s):
                wait(act, leaky, u + 1)
                nc.scalar.activation(work[:, s, :, :], work[:, s, :, :], ACT.Exp, scale=0.25).then_inc(probs, 1)

            def read_acc(k):
                wait(act, unit_done, TILES * (k + 1))
                nc.scalar.activation(acc_sb[:, :], acc_ps[:, 0:CN], ACT.Copy).then_inc(acc_read, 1)

            def head(b, c, first=False, last=False):
                for s in range(RING):
                    if s == RING - 1 and not first:
                        read_acc(K(b, c) - 1)
                    read_b(b, c, s, s)
                    step = 3 * (c - 1) + s - 1
                    if step in (1, 3, 5) and s and not last:
                        read_proj(b + 1, step // 2)
                    if not (first and s < 2):
                        exps(U(b, c, s) - 2, (s - 2) % RING)

            def steady(b, c):
                with act.Fori(1, GROUPS) as g:
                    for s in range(RING):
                        m = g * RING + s
                        read_b(b, c, m, s)
                        exps(U(b, c, m) - 2, (s - 2) % RING)

            def batch(b, last=False):
                steady(b, 0)
                for c in range(1, CHUNKS):
                    head(b, c, last=last)
                    steady(b, c)

            for k in range(CHUNKS):
                read_hT(act, 0, k)
                read_proj(0, k)
            head(0, 0, first=True)
            with act.Fori(0, B - 1) as b:
                batch(b)
                head(b + 1, 0)
            batch(B - 1, last=True)
            exps(U(B, 0, 0) - 2, RING - 2)
            exps(U(B, 0, 0) - 1, RING - 1)
            read_acc(B * CHUNKS - 1)

            with by_flag(act):
                all_stored(act)
                with act.Fori(0, B) as b:
                    for k in range(3):
                        wait(act, g_prep, 11 * b + k + 1)
                        nc.scalar.activation(hT[:, CN * k:CN * k + CN], prep_ps[0:F, 0:CN], ACT.Relu).then_inc(g_read, 1)
                    for n, to in enumerate((g_self, g_other)):
                        for k in range(3):
                            wait(act, g_prep, 11 * b + 3 * n + k + 4)
                            nc.scalar.activation(to[:, CN * k:CN * k + CN], prep_ps[0:F, 0:CN], ACT.Copy)\
                              .then_inc(g_read, 1)
                    for k in range(2):
                        wait(act, g_prep, 11 * b + k + 10)
                        half = TILES // 2
                        nc.scalar.activation(
                            g_feats[:, half * k:half * k + half, :, 0:D].rearrange("p m h o -> p (m h) o"),
                            prep_ps[0:P, 0:half * F].rearrange("p (t o) -> p t o", o=D), ACT.Copy).then_inc(g_read, 1)
                    with act.Fori(0, TILES) as i:
                        for h in range(H):
                            t = T(b, i)
                            q = H * t + h
                            wait(act, g_v, VS(t, h, "negate"))
                            nc.scalar.activation(g_prob, g_prob, ACT.Exp, bias=neg_max[:, :],
                                                 accum_out=row_sum[:, :]).then_inc(g_exp, 1)
                            wait(act, g_turn, q + 1)
                            nc.scalar.activation(g_turned.rearrange("p (a n) -> p a n", a=3), g_banks, ACT.Copy)\
                              .then_inc(g_copied, 1)

        @block.vector
        def _(dve):
            nc.vector.memset(zeros[:, :], 0.0).then_inc(zero_made, 1)
            nc.vector.memset(feats_f[:, :], 1.0).then_inc(zero_made, 1)
            nc.vector.memset(norms[:, :], 0.0).then_inc(zero_made, 1)

            def norm_sum(b):
                wait(dve, x_loaded, 16 * (b + 1))
                wait(dve, ln_g, 4 * b)
                xb = x_sb[:, :, :, :].rearrange("p b i f -> p (b i f)")[:, ds(b * (TILES * F), TILES * F)]\
                    .rearrange("p (i f) -> p i f", i=TILES)
                nc.vector.tensor_reduce(sums[:, :], xb, AX.X, ALU.add).then_inc(ln_v, 1)
                wait(dve, ln_v, 4 * b + 1)
                nc.vector.tensor_scalar(mean[:, :], sums[:, :], 1.0 / F, None, ALU.mult).then_inc(ln_v, 1)

            def norm_var(b):
                wait(dve, ln_g, 4 * b + 2)
                nc.vector.tensor_reduce(var_s[:, :], squared[:, :, :], AX.X, ALU.add).then_inc(ln_v, 1)
                wait(dve, ln_v, 4 * b + 3)
                nc.vector.tensor_scalar(var_e[:, :], var_s[:, :], 1.0 / F, EPS, ALU.mult, ALU.add).then_inc(ln_v, 1)

            def unit(b, c, m, s):
                u, n = U(b, c, m), heads_of_dve(s)
                wait(dve, a_ready, u + 1)
                wait(dve, unit_done, u - RING + 1)
                nc.vector.tensor_copy(work[:, s, 0:n, :], score_ps[:, s % 2:s % 2 + n, 0:CN]).then_inc(a_out, 1)

            def leak(u, s):
                wait(dve, a_out, u + 1)
                wait(dve, b_out, u + 1)
                w = work[:, s, :, :].rearrange("p h n -> p (h n)")
                nc.vector.scalar_tensor_tensor(w, w, SLOPE, w, ALU.mult, ALU.max).then_inc(leaky, 1)

            def chunk_end(b, c):
                n = 3 * (K(b, c) + 1)
                o = o_ps.rearrange("p j (h r) -> p j h r", h=H)
                wait(dve, o_made, K(b, c) + 1)
                wait(dve, stored, 16 * (K(b, c) + 1))
                nc.vector.tensor_scalar(den[:, :, :], o[:, :, :, D], TINY, None, ALU.max).then_inc(o_v, 1)
                wait(dve, o_v, n + 1)
                nc.vector.reciprocal(rec[:, :, :], den[:, :, :]).then_inc(o_v, 1)
                wait(dve, o_v, n + 2)
                nc.vector.tensor_tensor(res[:, :, :, :], o[:, :, :, 0:D],
                                        rec[:, :, :].unsqueeze(3).to_broadcast([P, JT, H, D]), ALU.mult)\
                  .then_inc(o_v, 1)

            def read_feats(b, k, first=False):
                half = TILES // 2
                wait(dve, prep_made, FEAT(b, k) + 1)
                if not first:
                    wait(dve, ring_ready, U(b - 1, 0, 0) + 1)
                if first:
                    dve.wait_ge(zero_made, 3)
                dst = feats_f[:, ds((b % 2) * (TILES * H * OC) + k * half * H * OC, half * H * OC)]\
                    .rearrange("p (t o) -> p t o", o=OC)[:, :, 0:D]
                nc.vector.tensor_copy(dst, prep_ps[0:P, 0:half * F].rearrange("p (t o) -> p t o", o=D))\
                  .then_inc(prep_read, 1)

            def read_norm(b):
                wait(dve, prep_made, NORM(b) + 1)
                nc.vector.tensor_reduce(norms[:, ds(b, 1)], prep_ps[0:96, 0:CN], AX.X, ALU.max).then_inc(prep_read, 1)

            def head(b, c, first=False, last=False):
                for s in range(RING):
                    unit(b, c, s, s)
                    if not (first and s == 0):
                        leak(U(b, c, s) - 1, (s - 1) % RING)
                    if c == 0 and s in (1, 2):
                        read_feats(b, s - 1, first)
                    if c == 0 and s == 3:
                        read_norm(b)
                    step = 3 * (c - 1) + s - 1
                    if step in (0, 2, 4) and s and not last:
                        read_hT(dve, b + 1, step // 2)
                if not first:
                    chunk_end(*((b - 1, CHUNKS - 1) if c == 0 else (b, c - 1)))

            def group(b, c, g):
                for s in range(RING):
                    unit(b, c, g * RING + s, s)
                    leak(U(b, c, g * RING + s) - 1, (s - 1) % RING)

            def steady(b, c):
                with dve.Fori(1, GROUPS) as g:
                    group(b, c, g)

            def batch(b, last=False):
                if not last:
                    norm_sum(b + 1)
                group(b, 0, 1)
                if not last:
                    norm_var(b + 1)
                group(b, 0, 2)
                for c in range(1, CHUNKS):
                    head(b, c, last=last)
                    steady(b, c)

            dve.sem_inc(o_v, 3)
            norm_sum(0)
            norm_centre(dve, 0)
            norm_var(0)
            norm_scale(dve, 0)
            for k in range(CHUNKS):
                split(dve, 0, k)
            dve.wait_ge(zero_made, 3)
            head(0, 0, first=True)
            with dve.Fori(0, B - 1) as b:
                batch(b)
                head(b + 1, 0)
            batch(B - 1, last=True)
            nc.vector.tensor_reduce(top[:, :], norms[:, :], AX.X, ALU.max).then_inc(top_v, 1)
            leak(U(B, 0, 0) - 1, RING - 1)
            dve.wait_ge(top_turned, 1)
            nc.vector.tensor_reduce(top_all[:, :], prep_ps[0:1, 0:96], AX.X, ALU.max).then_inc(top_v, 1)
            dve.wait_ge(top_v, 2)
            nc.vector.tensor_scalar(flag[:, :], top_all[:, :], SAFE, None, ALU.is_gt).then_inc(flag_made, 1)
            chunk_end(B - 1, CHUNKS - 1)
            dve.wait_ge(o_g, 3 * (B * CHUNKS - 1))
            finish(dve, B - 1, CHUNKS - 1)

            with by_flag(dve):
                all_stored(dve)
                with dve.Fori(0, B) as b:
                    n = 7 * b
                    xb = x_sb[:, :, :, :].rearrange("p b i f -> p (b i f)")[:, ds(b * (TILES * F), TILES * F)]\
                        .rearrange("p (i f) -> p i f", i=TILES)

                    def spread(stat):
                        return stat[:, :].unsqueeze(2).to_broadcast([P, TILES, F])

                    nc.vector.tensor_reduce(sums[:, :], xb, AX.X, ALU.add).then_inc(g_ln, 1)
                    wait(dve, g_ln, n + 1)
                    nc.vector.tensor_scalar(mean[:, :], sums[:, :], 1.0 / F, None, ALU.mult).then_inc(g_ln, 1)
                    wait(dve, g_ln, n + 2)
                    nc.vector.tensor_tensor(centred[:, :, :], xb, spread(mean), ALU.subtract).then_inc(g_ln, 1)
                    wait(dve, g_ln, n + 3)
                    nc.vector.tensor_tensor(squared[:, :, :], centred[:, :, :], centred[:, :, :], ALU.mult)\
                      .then_inc(g_ln, 1)
                    wait(dve, g_ln, n + 4)
                    nc.vector.tensor_reduce(var_s[:, :], squared[:, :, :], AX.X, ALU.add).then_inc(g_ln, 1)
                    wait(dve, g_ln, n + 5)
                    nc.vector.tensor_scalar(var_e[:, :], var_s[:, :], 1.0 / F, EPS, ALU.mult, ALU.add)\
                      .then_inc(g_ln, 1)
                    wait(dve, g_rstd, b + 1)
                    nc.vector.tensor_tensor(normed[:, :, :], centred[:, :, :], spread(rstd), ALU.mult)\
                      .then_inc(g_ln, 1)
                    wait(dve, g_read, 11 * b + 11)
                    dve.sem_inc(passed, 1)
                    with dve.Fori(0, TILES) as i:
                        t = T(b, i)
                        r = res[:, 0, :, :].rearrange("p h d -> p (h d)")
                        x_row = x_sb[:, :, :, :].rearrange("p b i f -> p (b i f)")[:, ds(t * F, F)]
                        wait(dve, g_loaded, 16 * (t + 1))
                        nc.vector.tensor_scalar(g_mask, g_adj, -1.0, MASKED, ALU.add, ALU.mult).then_inc(g_v, 1)
                        for h in range(H):
                            q = H * t + h

                            def done(step):
                                wait(dve, g_v, VS(t, h, step))

                            nc.vector.tensor_scalar(g_head, g_self[:, ds(P * i, P)], group_of[0:F, h:h + 1], None,
                                                    ALU.mult).then_inc(g_v, 1)
                            wait(dve, g_scores, q + 1)
                            nc.vector.tensor_tensor(g_prob.rearrange("p (a n) -> p a n", a=3), g_banks,
                                                    g_adj.rearrange("p (a n) -> p a n", a=3), ALU.mult).then_inc(g_v, 1)
                            done("adj")
                            nc.vector.scalar_tensor_tensor(g_prob, g_prob, SLOPE, g_prob, ALU.mult, ALU.max)\
                              .then_inc(g_v, 1)
                            done("leaky")
                            nc.vector.scalar_tensor_tensor(g_prob, g_prob, float(D) ** -0.5, g_mask, ALU.mult, ALU.add)\
                              .then_inc(g_v, 1)
                            done("mask")
                            nc.vector.tensor_reduce(row_max[:, :], g_prob, AX.X, ALU.max).then_inc(g_v, 1)
                            done("max")
                            nc.vector.tensor_scalar(neg_max[:, :], row_max[:, :], -1.0, None, ALU.mult).then_inc(g_v, 1)
                            wait(dve, g_exp, q + 1)
                            nc.vector.tensor_tensor(g_prob, g_prob, g_adj, ALU.mult).then_inc(g_v, 1)
                            nc.vector.reciprocal(row_rec[:, :], row_sum[:, :]).then_inc(g_v, 1)
                            done("recip")
                            wait(dve, g_out, q + 1)
                            nc.vector.tensor_scalar(res[:, 0, h, :], acc_ps[0:P, 0:D], row_rec[:, :], None, ALU.mult)\
                              .then_inc(g_v, 1)
                        end = TILE_STEPS * t + TILE_STEPS - 3
                        wait(dve, g_v, end)
                        nc.vector.tensor_tensor(r, r, bias_bc[:, :], ALU.add).then_inc(g_v, 1)
                        wait(dve, g_v, end + 1)
                        nc.vector.tensor_scalar(r, r, 0.0, None, ALU.max).then_inc(g_v, 1)
                        wait(dve, g_v, end + 2)
                        nc.vector.tensor_tensor(r, r, x_row, ALU.add).then_inc(g_v, 1)

        @block.tensor
        def _(pe):
            mm = nc.tensor.matmul

            def make_hT(b, k):
                wait(pe, prep_read, HT(b, k))
                if not isinstance(b, int):
                    pe.sem_inc(passed, 1)
                for j in range(JT):
                    ins = nc.tensor.transpose(prep_ps[0:F, P * j:P * j + P], normed[:, JT * k + j, :],
                                              ident_f[0:P, 0:P])
                ins.then_inc(prep_made, 1)

            def make_proj(b, k):
                wait(pe, prep_read, PROJ(b, k))
                mm(prep_ps[:, 0:CN], w_proj[:, :], hT[:, CN * k:CN * k + CN], start=True, stop=True)\
                    .then_inc(prep_made, 1)

            def make_feats(b, k):
                wait(pe, prep_read, FEAT(b, k))
                half = TILES // 2
                for t in range(half):
                    i = half * k + t
                    ins = mm(prep_ps[0:P, F * t:F * t + F], hT[:, P * i:P * i + P], w_f[:, :], start=True, stop=True)
                ins.then_inc(prep_made, 1)

            def make_norm(b):
                wait(pe, squared_g, CHUNKS * (b + 1))
                wait(pe, prep_read, NORM(b))
                for k in range(3):
                    ins = mm(prep_ps[32 * k:32 * k + 32, 0:CN], group_of[:, :], proj_sq[:, CN * k:CN * k + CN],
                             start=True, stop=True)
                ins.then_inc(prep_made, 1)

            def prep(b, step):
                if step % 2 == 0:
                    make_hT(b, step // 2)
                else:
                    make_proj(b, step // 2)

            def masked_scores(b, c, m, s, h):
                slot = (b % 2) * (H * N)
                bank = s % 2 if h == 0 else 2 if h == 1 and heads_of_dve(s) == 2 else 2 + h
                for j in range(JT):
                    mm(score_ps[:, bank, P * j:P * j + P], a_nat_f[:, ds((K(b, c) % 2) * (JT * N) + j * N + P * m, P)],
                       edge_or_big[:, :], start=j == 0, stop=j == 0, skip_group_check=True)
                return mm(score_ps[:, bank, 0:CN], other_f[:, ds(slot + h * N + P * m, P)],
                          self_f[:, ds(slot + h * N + CN * c, CN)], start=False, stop=True, skip_group_check=True)

            def scores_dve(b, c, m, s):
                wait(pe, a_out, U(b, c, m) - 1)
                for h in range(heads_of_dve(s)):
                    ins = masked_scores(b, c, m, s, h)
                ins.then_inc(a_ready, 1)

            def scores(b, c, m, s, in_head=False):
                u = U(b, c, m)
                if s == 0:
                    scores_dve(b, c, m, s)
                wait(pe, b_out, u)
                for h in range(heads_of_dve(s), H):
                    ins = masked_scores(b, c, m, s, h)
                ins.then_inc(b_ready, 1)
                if s < RING - 1:
                    if s + 1 == TWO_HEADS and not in_head:
                        wait(pe, o_v, 3 * (K(b, c) + 1))
                    scores_dve(b, c, m + 1, s + 1)

            def multiply(u, s, start=False, first=False):
                wait(pe, ring_ready, u + 1)
                wait(pe, probs, u + 1)
                if first:
                    mm(acc_ps[:, 0:CN], zeros[:, 0:128], zeros[:, 0:CN], start=True, stop=True)
                for h in range(H):
                    ins = mm(acc_ps[32 * h:32 * h + OC, 0:CN], ring_f[:, s, h, :], work[:, s, h, :],
                             start=start, stop=True, skip_group_check=True)
                ins.then_inc(unit_done, 1)

            def turn_acc(k, units):
                wait(pe, a_out, units)
                wait(pe, acc_read, k + 1)
                for j in range(JT):
                    ins = nc.tensor.transpose(o_ps[:, j, :], acc_sb[:, P * j:P * j + P], ident_f[:, :])
                ins.then_inc(o_made, 1)

            def head(b, c, first=False, last=False):
                k = K(b, c)
                wait(pe, adj_loaded, 32 * (k + 1))
                if c == 0:
                    wait(pe, parts_placed, PLACED if first else PLACED * (b + CHUNKS))
                for s in range(RING):
                    u = U(b, c, s)
                    if c == 1 and not last:
                        if s == 0:
                            wait(pe, ln_g, 4 * (b + 1) + 4)
                            pe.sem_inc(passed, 1)
                    scores(b, c, s, s, in_head=True)
                    if c == 0 and s in (1, 2):
                        make_feats(b, s - 1)
                    if c == 0 and s == 3:
                        make_norm(b)
                    if c and s and not last:
                        prep(b + 1, 3 * (c - 1) + s - 1)
                    if s < 3:
                        if not first:
                            multiply(u - 3, (s - 3) % RING)
                    else:
                        if not first:
                            turn_acc(k - 1, u)
                        multiply(u - 3, 0, start=True, first=first)

            def steady(b, c):
                with pe.Fori(1, GROUPS) as g:
                    if c == 0:
                        wait(pe, parts_placed, PLACED * (b + g + 1))
                    for s in range(RING):
                        m = g * RING + s
                        u = U(b, c, m)
                        scores(b, c, m, s)
                        multiply(u - 3, (s - 3) % RING)

            def batch(b, last=False):
                steady(b, 0)
                for c in range(1, CHUNKS):
                    head(b, c, last=last)
                    steady(b, c)

            pe.wait_ge(const_made, 10)
            pe.wait_ge(const_loaded, 64)
            pe.wait_ge(zero_made, 3)
            pe.wait_ge(ln_g, 4)
            for step in range(6):
                prep(0, step)
            pe.wait_ge(ones_placed, 16)
            head(0, 0, first=True)
            with pe.Fori(0, B - 1) as b:
                batch(b)
                head(b + 1, 0)
            batch(B - 1, last=True)
            pe.wait_ge(top_v, 1)
            mm(prep_ps[0:1, 0:96], top[:, :], ident_f[0:96, 0:96], start=True, stop=True).then_inc(top_turned, 1)
            for s in range(1, RING):
                multiply(U(B, 0, 0) - RING + s, s)
            turn_acc(B * CHUNKS - 1, UNITS * B)

            with by_flag(pe):
                all_stored(pe)
                def free(n):
                    wait(pe, g_read, n)
                    pe.sem_inc(passed, 1)

                with pe.Fori(0, B) as b:
                    wait(pe, g_ln, 7 * b + 7)
                    pe.sem_inc(passed, 1)
                    for k in range(3):
                        if k:
                            free(11 * b + k)
                        for j in range(JT):
                            ins = nc.tensor.transpose(prep_ps[0:F, P * j:P * j + P], normed[:, JT * k + j, :],
                                                      ident_f[0:P, 0:P])
                        ins.then_inc(g_prep, 1)
                    for n in range(2):
                        for k in range(3):
                            free(11 * b + 3 * n + k + 3)
                            mm(prep_ps[0:F, 0:CN], w_proj[:, F * n:F * n + F], hT[:, CN * k:CN * k + CN],
                               start=True, stop=True).then_inc(g_prep, 1)
                    for k in range(2):
                        free(11 * b + k + 9)
                        half = TILES // 2
                        for j in range(half):
                            i = half * k + j
                            ins = mm(prep_ps[0:P, F * j:F * j + F], hT[:, P * i:P * i + P], w_f[:, :],
                                     start=True, stop=True)
                        ins.then_inc(g_prep, 1)
                    with pe.Fori(0, TILES) as i:
                        t = T(b, i)
                        for h in range(H):
                            q = H * t + h
                            wait(pe, g_v, VS(t, h, "select"))
                            for n in range(3):
                                ins = mm(g_banks[:, n, :], g_head, g_other[:, CN * n:CN * n + CN], start=True, stop=True)
                            ins.then_inc(g_scores, 1)
                            wait(pe, g_v, VS(t, h, "keep"))
                            for m in range(TILES):
                                ins = nc.tensor.transpose(g_banks[:, m // JT, P * (m % JT):P * (m % JT) + P],
                                                          g_prob[:, P * m:P * m + P], ident_f[0:P, 0:P])
                            ins.then_inc(g_turn, 1)
                            wait(pe, g_copied, q + 1)
                            for m in range(TILES):
                                ins = mm(acc_ps[0:P, 0:D], g_turned[:, P * m:P * m + P], g_feats[:, m, h, 0:D],
                                         start=m == 0, stop=m == TILES - 1)
                            ins.then_inc(g_out, 1)


_INS = ["x", "adj", "L0_gnn_kernel", "L0_gnn_attention_kernel", "L0_gnn_attention_kernel_2", "L0_gnn_bias"]


def kernel(**inputs):
    import concourse.bacc as bacc
    from concourse import mybir
    from concourse.bass_utils import run_bass_kernel_spmd as run

    nc = bacc.Bacc("TRN2", target_bir_lowering=False, num_devices=1)
    arrays, args = {}, []
    for name in _INS:
        a = np.ascontiguousarray(inputs[name])
        arrays[name] = a
        args.append(nc.dram_tensor(name, a.shape, mybir.dt.from_np(a.dtype), kind="ExternalInput").ap())
    args.append(nc.dram_tensor("out", (B, N, H * D), mybir.dt.float32, kind="ExternalOutput").ap())
    gat_program(nc, *args)
    r = run(nc, [arrays], core_ids=[0])
    return r.results[0]["out"]
```
